# Optimizing a Trainium2 kernel written in Bass

```python
import numpy as np
import jax
import jax.numpy as jnp

def _softmax(x, axis=-1):
    return jax.nn.softmax(x, axis=axis)

def _gelu(x):
    return jax.nn.gelu(x, approximate=True)

def _silu(x):
    return jax.nn.silu(x)

def _sigmoid(x):
    return jax.nn.sigmoid(x)

def _layernorm(x, axis=-1, eps=1e-05):
    m = jnp.mean(x, axis=axis, keepdims=True)
    v = jnp.var(x, axis=axis, keepdims=True)
    return (x - m) / jnp.sqrt(v + eps)

def _scatter_add(tgt, idx, src, axis=0):
    return tgt.at[idx].add(src)

def _segment_sum(src, seg, n):
    return jax.ops.segment_sum(src, seg, n)
kernel_name = 'mk_recurrent_d1_jaxref_r2_c6a7a2'

def setup_inputs(seed: int=0):
    np.random.seed(seed)
    _w = jnp.asarray

    def _L0_attn_setup():
        import jax, jax.numpy as jnp
        import numpy as np
        B, T, D = (4, 1024, 512)
        key = jax.random.key(seed)
        kx, kq, kk, kv = jax.random.split(key, 4)
        scale = 1.0 / np.sqrt(D)
        return {'x': jax.random.normal(kx, (B, T, D), dtype=jnp.float32), 'Wq': jax.random.normal(kq, (D, D), dtype=jnp.float32) * scale, 'Wk': jax.random.normal(kk, (D, D), dtype=jnp.float32) * scale, 'Wv': jax.random.normal(kv, (D, D), dtype=jnp.float32) * scale}
    _L0_attn_in = _L0_attn_setup()

    def _L0_ffn_setup():
        import jax, jax.numpy as jnp
        import numpy as np
        H = 512
        RH = 256
        E = 16
        B, S = (4, 1024)
        TEMP = 1.0
        key = jax.random.key(seed)
        ks = jax.random.split(key, 12)
        sc = lambda fan_in: 1.0 / np.sqrt(fan_in)
        return {'hidden_states': jax.random.normal(ks[0], (B, S, H), dtype=jnp.float32), 'W1': jax.random.uniform(ks[1], (H, RH), jnp.float32, -sc(H), sc(H)), 'b1': jax.random.uniform(ks[2], (RH,), jnp.float32, -sc(H), sc(H)), 'W2': jax.random.uniform(ks[3], (RH, E), jnp.float32, -sc(RH), sc(RH)), 'b2': jax.random.uniform(ks[4], (E,), jnp.float32, -sc(RH), sc(RH)), 'Wg1': jax.random.uniform(ks[5], (H, RH), jnp.float32, -sc(H), sc(H)), 'bg1': jax.random.uniform(ks[6], (RH,), jnp.float32, -sc(H), sc(H)), 'Wg2': jax.random.uniform(ks[7], (RH, 1), jnp.float32, -sc(RH), sc(RH)), 'bg2': jax.random.uniform(ks[8], (1,), jnp.float32, -sc(RH), sc(RH)), 'expert_scales': jax.random.normal(ks[9], (E, H), dtype=jnp.float32), 'expert_biases': jax.random.normal(ks[10], (E, H), dtype=jnp.float32)}
    _L0_ffn_in = _L0_ffn_setup()
    _d = {'L0_attn_x': _L0_attn_in['x'], 'L0_attn_Wq': _L0_attn_in['Wq'], 'L0_attn_Wk': _L0_attn_in['Wk'], 'L0_attn_Wv': _L0_attn_in['Wv'], 'L0_ffn_W1': _L0_ffn_in['W1'], 'L0_ffn_b1': _L0_ffn_in['b1'], 'L0_ffn_W2': _L0_ffn_in['W2'], 'L0_ffn_b2': _L0_ffn_in['b2'], 'L0_ffn_Wg1': _L0_ffn_in['Wg1'], 'L0_ffn_bg1': _L0_ffn_in['bg1'], 'L0_ffn_Wg2': _L0_ffn_in['Wg2'], 'L0_ffn_bg2': _L0_ffn_in['bg2'], 'L0_ffn_expert_scales': _L0_ffn_in['expert_scales'], 'L0_ffn_expert_biases': _L0_ffn_in['expert_biases']}
    _x0 = _d['L0_attn_x']
    _d['L0_attn_x'] = jax.random.normal(jax.random.fold_in(jax.random.key(seed), 1), (8, 1024, 512), dtype=_x0.dtype)
    del _x0
    return _d

def reference(L0_attn_x, L0_attn_Wq, L0_attn_Wk, L0_attn_Wv, L0_ffn_W1, L0_ffn_b1, L0_ffn_W2, L0_ffn_b2, L0_ffn_Wg1, L0_ffn_bg1, L0_ffn_Wg2, L0_ffn_bg2, L0_ffn_expert_scales, L0_ffn_expert_biases):

    def _L0_attn_ref(x, Wq, Wk, Wv):
        import jax, jax.numpy as jnp
        import numpy as np
        B, T, D = (4, 1024, 512)
        q = jnp.einsum('btd,od->bto', x, Wq)
        k = jnp.einsum('btd,od->bto', x, Wk)
        v = jnp.einsum('btd,od->bto', x, Wv)
        scores = jnp.einsum('bqd,bkd->bqk', q, k)
        inv_sqrt_d = 1.0 / np.sqrt(k.shape[-1]).astype(np.float32)
        weights = jax.nn.softmax(scores * inv_sqrt_d, axis=-1)
        return jnp.einsum('bqk,bkd->bqd', weights, v)

    def _L0_ffn_ref(hidden_states, W1, b1, W2, b2, Wg1, bg1, Wg2, bg2, expert_scales, expert_biases):
        import jax, jax.numpy as jnp
        import numpy as np
        H = 512
        RH = 256
        E = 16
        B, S = (4, 1024)
        TEMP = 1.0
        b, s, h = hidden_states.shape
        flat = hidden_states.reshape(-1, h)
        routing_scores = jax.nn.relu(flat @ W1 + b1) @ W2 + b2
        routing_scores = routing_scores / TEMP
        gate = jax.nn.sigmoid(jnp.tanh(flat @ Wg1 + bg1) @ Wg2 + bg2)
        routing_scores = routing_scores * gate
        expert_probs = jax.nn.softmax(routing_scores, axis=-1)
        top_idx = jnp.argmax(expert_probs, axis=-1)
        scales = expert_scales[top_idx]
        biases = expert_biases[top_idx]
        routed = flat * scales + biases
        return routed.reshape(b, s, h)
    x = L0_attn_x
    xn = _layernorm(x, axis=-1)
    s = _L0_attn_ref(xn, L0_attn_Wq, L0_attn_Wk, L0_attn_Wv)
    g = _silu(_L0_ffn_ref(xn, L0_ffn_W1, L0_ffn_b1, L0_ffn_W2, L0_ffn_b2, L0_ffn_Wg1, L0_ffn_bg1, L0_ffn_Wg2, L0_ffn_bg2, L0_ffn_expert_scales, L0_ffn_expert_biases))
    x = x + s * g
    return x

_drawn_inputs = setup_inputs


def setup_inputs(seed=0):
    import zlib

    import numpy as np

    out = dict(_drawn_inputs(seed))
    spreads = {}
    factors = {'L0_ffn_b1': 3.386}
    for name, (base, spread) in spreads.items():
        noise = np.random.default_rng([zlib.crc32(name.encode()), seed]).standard_normal(out[name].shape)
        drawn = base * np.exp(spread * noise) if base else spread * noise
        out[name] = jnp.asarray(drawn.astype(out[name].dtype))
    for name, factor in factors.items():
        out[name] = (out[name] * factor).astype(out[name].dtype)
    return out
```

```python
from contextlib import ExitStack

import concourse.bass as bass
from concourse import mybir

F32 = mybir.dt.float32
F32R = mybir.dt.float32r
BF16 = mybir.dt.bfloat16
ALU = mybir.AluOpType
ACT = mybir.ActivationFunctionType
AX = mybir.AxisListType

P = 128
BANK = 512
EPS = 1e-5


def routed_attention_block(nc, x, Wq, Wk, Wv, W1, b1, W2, b2, Wg1, bg1, Wg2, bg2, scales, biases, out):
    B, T, D = x.shape
    RH = W1.shape[1]
    E = W2.shape[1]
    KC = D // P
    NT = T // P
    NH = T // BANK
    TH = NT // NH
    HC = 2 * RH // P
    SCALE = 1.0 / float(D) ** 0.5
    assert D == BANK and T == 2 * BANK and RH == 2 * P and E == 16

    XT_U = KC * NH
    H_U = HC * NH
    Y_U = KC * NH
    V_U = NT
    U = H_U + Y_U + V_U
    LO = 32
    SMALL = HC + HC + 2 + 6
    EC = 3 * 32

    x_t = x.rearrange("b (t p) d -> (b t) p d", p=P)
    out_t = out.rearrange("b (t p) d -> (b t) p d", p=P)

    units = []
    for n in range(NH):
        units += [("h", n, c) for c in range(HC)] + [("y", n, c) for c in range(KC)]
    units += [("v", t, 0) for t in range(NT)]
    rank = []
    for u, (kind, _, _) in enumerate(units):
        rank.append(sum(k == kind for k, _, _ in units[:u + 1]))
    last_h = [max(u for u, (k, n, _) in enumerate(units) if k == "h" and n == half) for half in range(NH)]

    with ExitStack() as ctx:
        def sb(name, shape, dt, where=ctx):
            return where.enter_context(nc.sbuf_tensor(name, shape, dt))

        def sem(name):
            return ctx.enter_context(nc.semaphore(name))

        w1g = [sb(f"w1g_{p}", [P, KC, 2 * RH], F32R) for p in ("hi", "lo")]
        A = [sb(f"A_{p}", [P, KC, D], F32R) for p in ("hi", "lo")]
        WvT = [sb(f"WvT_{p}", [P, KC, D], F32R) for p in ("hi", "lo")]
        xnT = [sb(f"xnT_{p}", [P, KC, T], F32R) for p in ("hi", "lo")]
        PT = [sb(f"PT_{p}", [P, NT, P], F32R) for p in ("hi", "lo")]
        w2s = sb("w2s", [P, HC, P], F32R)
        table = sb("table", [EC, 2 * D], BF16)
        ident = sb("ident", [P, P], F32)
        identb = sb("identb", [P, P], BF16)
        xstage = sb("xstage", [P, 2, D], F32)
        xres = sb("xres", [P, 2, D], F32)
        xn = sb("xn", [P, NT, D], F32)
        Pr = sb("Pr", [P, T], F32)
        G = sb("G", [P, 2, D], F32)
        h = sb("h", [P, 2, BANK], F32)
        th = h[:, 0, :]
        hs = [sb(f"h_{p}", [P, 2, BANK], F32R) for p in ("hi", "lo")]
        Rs = G[:, 1, :]
        Z = G[:, 0, :].rearrange("p (t r) -> p t r", t=NT)
        z = sb("z", [P, NT, E + 1], F32)
        rs = sb("rs", [P, NT, E], F32)
        onehot = sb("onehot", [P, NT, EC], BF16)
        onehotT = sb("onehotT", [EC, T], BF16)
        b2g = sb("b2g", [P, E + 1], F32)
        rev = sb("rev", [P, E], F32)
        bcol = sb("bcol", [P, HC], F32)
        st = sb("st", [P, 2, 6], F32)
        mv = sb("mv", [P, 2, 2], F32)
        rstd = sb("rstd", [P, 2, 2], F32)
        epsc = sb("epsc", [P, 2], F32)
        mx = sb("mx", [P, 2, 2], F32)
        den = sb("den", [P, 2, 3], F32)
        gt = sb("gt", [P, 3, NT], F32)
        sm = sb("sm", [P, 4, NT], F32)

        S = ctx.enter_context(nc.psum_tensor("S", [P, NH, BANK], F32))
        Tp = ctx.enter_context(nc.psum_tensor("Tp", [P, NH, BANK], F32))
        O = ctx.enter_context(nc.psum_tensor("O", [P, BANK], F32))
        M = ctx.enter_context(nc.psum_tensor("M", [P, 2, BANK], F32))
        M2 = ctx.enter_context(nc.psum_tensor("M2", [P, BANK], F32))
        Mb = M2[:].bitcast(BF16)

        def unit_bank(u):
            return (S[:, u % 4, :] if u % 4 < 2 else Tp[:, u % 4 - 2, :])

        def xt_bank(v):
            return M[:, v % 3, :] if v % 3 < 2 else M2[:, :]

        ident_ready = sem("ident_ready")
        consts_set = sem("consts_set")
        small_loaded = sem("small_loaded")
        w_loaded = [sem(f"w_loaded{i}") for i in range(4)]
        w_hi = sem("w_hi")
        w1_split = sem("w1_split")
        qk_split = sem("qk_split")
        w2_split = sem("w2_split")
        b_zeroed = sem("b_zeroed")
        table_step = sem("table_step")
        table_ready = sem("table_ready")
        pre_full = sem("pre_full")
        pre_hi = sem("pre_hi")
        pre_split = sem("pre_split")
        x_loaded = [sem(f"x_loaded{i}") for i in range(2)]
        stats_done = sem("stats_done")
        moments_done = sem("moments_done")
        var_eps = sem("var_eps")
        rstd_done = sem("rstd_done")
        normed = sem("normed")
        xt_full = sem("xt_full")
        xt_hi = sem("xt_hi")
        xt_split = sem("xt_split")
        unit_full = sem("unit_full")
        act_done = sem("act_done")
        h_hi = sem("h_hi")
        h_split = sem("h_split")
        yv_hi = sem("yv_hi")
        yv_split = sem("yv_split")
        r_full = sem("r_full")
        r_copied = sem("r_copied")
        z_copied = sem("z_copied")
        rt_full = sem("rt_full")
        z_ready = sem("z_ready")
        gate_exp = sem("gate_exp")
        route = sem("route")
        route_sub = sem("route_sub")
        route_exp = sem("route_exp")
        onehot_ready = sem("onehot_ready")
        ot_full = sem("ot_full")
        ot_ready = sem("ot_ready")
        gathered = sem("gathered")
        scaled = sem("scaled")
        routed = sem("routed")
        tanh_done = sem("tanh_done")
        gate_ready = sem("gate_ready")
        s_full = sem("s_full")
        max_done = sem("max_done")
        negmax = sem("negmax")
        p_ready = sem("p_ready")
        pt_full = sem("pt_full")
        pt_hi = sem("pt_hi")
        pt_split = sem("pt_split")
        pv_half = sem("pv_half")
        o_full = sem("o_full")
        den_step = sem("den_step")
        f_done = sem("f_done")
        xres_loaded = [sem(f"xres_loaded{i}") for i in range(2)]
        out_built = sem("out_built")
        stored = sem("stored")

        setup = ExitStack()
        wraw = sb("wraw", [P, 4, KC, D], F32, setup)
        qs = [sb(f"Wq_{p}", [P, KC, D], F32R, setup) for p in ("hi", "lo")]
        ks = [sb(f"Wk_{p}", [P, KC, D], F32R, setup) for p in ("hi", "lo")]
        setup.close()
        yT = [sb(f"yT_{p}", [P, KC, T], F32R) for p in ("hi", "lo")]
        V = [sb(f"V_{p}", [P, NT, D], F32R) for p in ("hi", "lo")]
        w2raw = th[:, 0:HC * LO].rearrange("p (c e) -> p c e", c=HC)
        traw = Pr[0:EC, :]

        SPLIT3 = ((0, 0), (0, 1), (1, 0))

        block = ctx.enter_context(nc.Block())

        @block.sync
        def _(sp):
            def load_stage(t, slot, free):
                if free is not None:
                    sp.wait_ge(normed, free)
                sp.dma_start(xstage[:, slot, :], x_t[t] if isinstance(t, int) else
                             x_t[bass.ds(t, 1)].rearrange("a p d -> p (a d)")).then_inc(x_loaded[slot], 16)

            def load_res(t, slot):
                sp.dma_start(xres[:, slot, :], x_t[t] if isinstance(t, int) else
                             x_t[bass.ds(t, 1)].rearrange("a p d -> p (a d)")).then_inc(xres_loaded[slot], 16)

            for t in range(NT):
                load_stage(t, t % 2, t - 1 if t >= 2 else None)
            for t in range(2):
                load_res(t, t)
            sp.wait_ge(b_zeroed, 1)
            for c in range(HC // 2):
                sp.dma_start(w2raw[:, c, 0:E], W2[c * P:(c + 1) * P, :]).then_inc(small_loaded, 16)
                sp.dma_start(w2raw[:, HC // 2 + c, E:E + 1], Wg2[c * P:(c + 1) * P, :]).then_inc(small_loaded, 16)

            def body(b, last):
                if not last:
                    load_stage(b * NT + NT, 0, b * NT + NT - 1)
                    load_stage(b * NT + NT + 1, 1, b * NT + NT)
                for i in range(NT):
                    if not last and i + 2 < NT:
                        load_stage(b * NT + NT + i + 2, i % 2, b * NT + NT + i + 1)
                    sp.wait_ge(out_built, b * NT + i + 1)
                    sp.dma_start(out_t[b * NT + i] if isinstance(b, int) else
                                 out_t[bass.ds(b * NT + i, 1)].rearrange("a p d -> p (a d)"),
                                 xres[:, i % 2, :]).then_inc(stored, 16)
                    if not (last and i >= NT - 2):
                        sp.wait_ge(stored, (b * NT + i + 1) * 16)
                        load_res(b * NT + i + 2, i % 2)

            with sp.Fori(0, B - 1) as b:
                body(b, False)
            body(B - 1, True)
            sp.wait_ge(stored, B * NT * 16)

        @block.gpsimd
        def _(pool):
            pool.memset(ident[:], 0.0).then_inc(consts_set, 1)
            pool.wait_ge(consts_set, 1)
            pool.affine_select(out=ident[:], in_=ident[:], compare_op=ALU.not_equal, fill=1.0, base=0,
                               pattern=[[-1, P]], channel_multiplier=1).then_inc(ident_ready, 1)
            pool.memset(epsc[:, 0:1], EPS)
            pool.memset(epsc[:, 1:2], -0.5).then_inc(consts_set, 1)
            pool.wait_ge(consts_set, 2)
            pool.wait_ge(ident_ready, 1)
            pool.tensor_copy(identb[:], ident[:]).then_inc(ident_ready, 1)

            def invert_std(n, slot):
                pool.wait_ge(moments_done, n + 1)
                pool.tensor_tensor(rstd[:, slot, 0:1], mv[:, slot, 1:2], epsc[:, 0:1], ALU.add).then_inc(var_eps, 1)
                pool.wait_ge(var_eps, n + 1)
                pool.tensor_tensor(rstd[:, slot, 1:2], rstd[:, slot, 0:1], epsc[:, 1:2], ALU.pow).then_inc(rstd_done, 1)

            for t in range(NT):
                invert_std(t, t % 2)
            for n, part in enumerate((qs, ks)):
                pool.wait_ge(w_hi, n + 2)
                pool.tensor_tensor(part[1][:], wraw[:, n + 1], part[0][:].bitcast(F32), ALU.subtract).then_inc(qk_split, 1)
            pool.wait_ge(small_loaded, 16 * SMALL)
            pool.wait_ge(qk_split, 2)
            steps = 0

            def step(ins):
                nonlocal steps
                ins.then_inc(table_step, 1)
                steps += 1
                pool.wait_ge(table_step, steps)

            step(pool.tensor_copy(table[:], traw))
            for part in (1, 2):
                for r in range(32 * part, EC, 32):
                    step(pool.tensor_tensor(traw[r:r + 32], traw[r:r + 32], table[r:r + 32, :], ALU.subtract))
                    step(pool.tensor_copy(table[r:r + 32, :], traw[r:r + 32]))
            pool.memset(epsc[:, 0:1], EPS).then_inc(table_ready, 1)

            def body(b):
                for i in range(NT):
                    invert_std(b * NT + NT + i, i % 2)

            with pool.Fori(0, B - 1) as b:
                body(b)

        @block.scalar
        def _(act):
            def load(i, src, dst):
                act.dma_start(dst, src.rearrange("(k p) d -> p k d", p=P)).then_inc(w_loaded[i], 16)
            load(0, W1, wraw[:, 0, :, 0:RH])
            load(0, Wg1, wraw[:, 0, :, RH:])
            load(1, Wq, wraw[:, 1])
            load(2, Wk, wraw[:, 2])
            load(3, Wv, wraw[:, 3])
            for c in range(HC // 2):
                col = slice(c * P, (c + 1) * P)
                act.dma_start(bcol[:, c:c + 1], b1[col].rearrange("(p o) -> p o", o=1)).then_inc(small_loaded, 16)
                act.dma_start(bcol[:, HC // 2 + c:HC // 2 + c + 1],
                              bg1[col].rearrange("(p o) -> p o", o=1)).then_inc(small_loaded, 16)
            act.dma_start(b2g[:, 0:E], b2.partition_broadcast(P)).then_inc(small_loaded, 16)
            act.dma_start(b2g[:, E:E + 1], bg2.partition_broadcast(P)).then_inc(small_loaded, 16)
            act.wait_ge(b_zeroed, 1)
            for part in range(3):
                act.dma_start(traw[32 * part:32 * part + E, 0:D], scales).then_inc(small_loaded, 16)
                act.dma_start(traw[32 * part:32 * part + E, D:], biases).then_inc(small_loaded, 16)

            def split_hi(dst, src, done):
                act.activation(dst, src, ACT.Copy).then_inc(done, 1)

            for n, (part, need) in enumerate(((w1g, 32), (qs, 16), (ks, 16))):
                act.wait_ge(w_loaded[n], need)
                split_hi(part[0][:], wraw[:, n], w_hi)

            def xt_units(n0, lot, half):
                for v in lot:
                    act.wait_ge(xt_full, n0 + v + 1)
                    split_hi(xnT[0][:, v % KC, half * BANK:half * BANK + BANK], xt_bank(v), xt_hi)

            xt_units(0, range(0, KC), 0)
            xt_units(0, range(KC, XT_U), 1)
            for v in range(2 * KC):
                act.wait_ge(pre_full, v + 1)
                split_hi((WvT if v < KC else A)[0][:, v % KC, :], unit_bank(v), pre_hi)
            act.wait_ge(small_loaded, 16 * SMALL)

            def softmax_exp(b, i):
                act.wait_ge(negmax, b * NT + i + 1)
                act.activation(Pr[:], S[:].rearrange("p n c -> p (n c)"), ACT.Exp, bias=mx[:, i % 2, 1:2],
                               scale=SCALE, accum_out=den[:, i % 2, 0:1]).then_inc(p_ready, 1)

            def gate_tanh(b, i):
                act.wait_ge(routed, b * NT + i + 1)
                act.activation(th, G[:, i % 2, :], ACT.Tanh, scale=0.5).then_inc(tanh_done, 1)

            def pt_units(b, i):
                for n in range(NH):
                    act.wait_ge(pt_full, (b * NT + i) * NH + n + 1)
                    if i == NT - 1:
                        if n == 0:
                            act.wait_ge(pv_half, b + 1)
                        else:
                            act.wait_ge(o_full, b * NT + NT - 1)
                    split_hi(PT[0][:, n * TH:(n + 1) * TH, :].rearrange("p t c -> p (t c)"), Tp[:, n, :], pt_hi)

            def body(b, last):
                for u, (kind, n, c) in enumerate(units):
                    act.wait_ge(unit_full, b * U + u + 1)
                    if kind == "h":
                        r = rank[u]
                        if r > 2:
                            act.wait_ge(h_split, b * H_U + r - 2)
                        act.activation(h[:, (r - 1) % 2, :], unit_bank(u), ACT.Relu if c < HC // 2 else ACT.Tanh,
                                       bias=bcol[:, c:c + 1]).then_inc(act_done, 1)
                        act.wait_ge(act_done, b * H_U + r)
                        split_hi(hs[0][:, (r - 1) % 2, :], h[:, (r - 1) % 2, :], h_hi)
                    elif kind == "y":
                        split_hi(yT[0][:, c, n * BANK:(n + 1) * BANK], unit_bank(u), yv_hi)
                    else:
                        split_hi(V[0][:, n, :], unit_bank(u), yv_hi)
                    if u == last_h[1] + 3:
                        act.wait_ge(z_ready, b + 1)
                        act.activation(gt[:, 0, :], z[:, :, E], ACT.Exp, scale=-1.0).then_inc(gate_exp, 1)
                    if u == last_h[1] + 5:
                        act.wait_ge(route_sub, b + 1)
                        act.activation(rs[:], rs[:], ACT.Exp).then_inc(route_exp, 1)
                act.wait_ge(ot_full, b + 1)
                act.activation(onehotT[:], Mb[0:EC, :], ACT.Copy).then_inc(ot_ready, 1)
                gate_tanh(b, 0)
                softmax_exp(b, 0)
                for i in range(NT):
                    pt_units(b, i)
                    if i + 1 < NT:
                        gate_tanh(b, i + 1)
                        softmax_exp(b, i + 1)
                    if not last and i == NT - 2:
                        xt_units(b * XT_U + XT_U, range(0, KC), 0)
                    if not last and i == NT - 1:
                        xt_units(b * XT_U + XT_U, range(KC, XT_U), 1)

            with act.Fori(0, B - 1) as b:
                body(b, False)
            body(B - 1, True)

        @block.vector
        def _(dve):
            def layernorm_moments(b, t):
                n, slot = b * NT + t, t % 2
                dve.wait_ge(x_loaded[slot], b * (NT // 2 * 16) + (t // 2 + 1) * 16)
                dve.bn_stats(st[:, slot, :], xstage[:, slot, :]).then_inc(stats_done, 1)
                dve.wait_ge(stats_done, n + 1)
                dve.memset(sm[:, 3, 0:1], 0.0)
                dve.bn_aggr(mv[:, slot, :], st[:, slot, :]).then_inc(moments_done, 1)

            def layernorm_apply(n, t):
                dve.wait_ge(rstd_done, n + 1)
                dve.tensor_scalar(xn[:, t, :], xstage[:, t % 2, :], mv[:, t % 2, 0:1], rstd[:, t % 2, 1:2],
                                  ALU.subtract, ALU.mult).then_inc(normed, 1)

            def split_lo(dst, src, hi, done):
                dve.tensor_tensor(dst, src, hi.bitcast(F32), ALU.subtract).then_inc(done, 1)

            def xt_units(n0, lot, half):
                for v in lot:
                    dve.wait_ge(xt_hi, n0 + v + 1)
                    sl = slice(half * BANK, half * BANK + BANK)
                    split_lo(xnT[1][:, v % KC, sl], xt_bank(v), xnT[0][:, v % KC, sl], xt_split)

            dve.memset(th, 0.0)
            dve.memset(Pr[:], 0.0).then_inc(b_zeroed, 1)
            for t in range(2):
                layernorm_moments(0, t)
            for t in range(NT):
                layernorm_apply(t, t)
                if t + 2 < NT:
                    layernorm_moments(0, t + 2)
            dve.wait_ge(w_hi, 1)
            split_lo(w1g[1][:], wraw[:, 0], w1g[0][:], w1_split)
            xt_units(0, range(0, KC), 0)
            xt_units(0, range(KC, XT_U), 1)
            for v in range(2 * KC):
                dve.wait_ge(pre_hi, v + 1)
                W = WvT if v < KC else A
                split_lo(W[1][:, v % KC, :], unit_bank(v), W[0][:, v % KC, :], pre_split)
            dve.memset(w2s[:].bitcast(F32), 0.0)
            dve.memset(onehot[:], 0.0)
            for e in range(E):
                dve.memset(rev[:, e:e + 1], float(E - e)).then_inc(w2_split, 1)
            dve.wait_ge(small_loaded, 16 * SMALL)
            dve.wait_ge(w2_split, E)
            dve.tensor_copy(w2s[:, :, 0:LO], w2raw).then_inc(w2_split, 1)
            dve.wait_ge(w2_split, E + 1)
            split_lo(w2s[:, :, LO:2 * LO], w2raw, w2s[:, :, 0:LO], w2_split)

            def routing(b):
                STEPS = 12
                done = [b * STEPS]

                def step(ins, sem_=None):
                    ins.then_inc(route, 1)
                    done[0] = done[0] + 1
                    dve.wait_ge(route, done[0])

                def over_tiles(row):
                    return row.unsqueeze(2).to_broadcast([P, NT, E])

                step(dve.tensor_tensor(z[:], Z[:, :, 0:E + 1], Z[:, :, LO:LO + E + 1], ALU.add))
                dve.tensor_tensor(z[:], z[:], b2g[:].unsqueeze(1).to_broadcast([P, NT, E + 1]),
                                  ALU.add).then_inc(z_ready, 1)
                dve.wait_ge(gate_exp, b + 1)
                step(dve.tensor_scalar(gt[:, 1, :], gt[:, 0, :], 1.0, None, ALU.add))
                step(dve.reciprocal(gt[:, 2, :], gt[:, 1, :]))
                step(dve.tensor_tensor(rs[:], z[:, :, 0:E], over_tiles(gt[:, 2, :]), ALU.mult))
                step(dve.tensor_reduce(sm[:, 0, :], rs[:], AX.X, ALU.max))
                dve.tensor_tensor(rs[:], rs[:], over_tiles(sm[:, 0, :]), ALU.subtract).then_inc(route_sub, 1)

            def routing_pick(b):
                STEPS = 12
                done = [b * STEPS + 5]

                def step(ins):
                    ins.then_inc(route, 1)
                    done[0] = done[0] + 1
                    dve.wait_ge(route, done[0])

                def over_tiles(row):
                    return row.unsqueeze(2).to_broadcast([P, NT, E])

                dve.wait_ge(route_exp, b + 1)
                step(dve.tensor_reduce(sm[:, 1, :], rs[:], AX.X, ALU.add))
                step(dve.reciprocal(sm[:, 2, :], sm[:, 1, :]))
                step(dve.tensor_tensor(rs[:], rs[:], over_tiles(sm[:, 2, :]), ALU.mult))
                step(dve.tensor_reduce(sm[:, 0, :], rs[:], AX.X, ALU.max))
                step(dve.tensor_tensor(rs[:], rs[:], over_tiles(sm[:, 0, :]), ALU.is_ge))
                step(dve.tensor_tensor(rs[:], rs[:], rev[:].unsqueeze(1).to_broadcast([P, NT, E]), ALU.mult))
                step(dve.tensor_reduce(sm[:, 1, :], rs[:], AX.X, ALU.max))
                for part in range(3):
                    ins = dve.tensor_tensor(onehot[:, :, 32 * part:32 * part + E], rs[:], over_tiles(sm[:, 1, :]), ALU.is_equal)
                ins.then_inc(onehot_ready, 1)

            def route_tile(b, i):
                dve.wait_ge(gathered, b * NT + i + 1)
                if i >= 2:
                    dve.wait_ge(out_built, b * NT + i - 1)
                dve.tensor_tensor(G[:, i % 2, :], M[:, 0, :], xn[:, i, :], ALU.mult).then_inc(scaled, 1)
                dve.wait_ge(scaled, b * NT + i + 1)
                dve.tensor_tensor(G[:, i % 2, :], G[:, i % 2, :], M[:, 1, :], ALU.add).then_inc(routed, 1)

            def gate_tile(b, i):
                dve.wait_ge(tanh_done, b * NT + i + 1)
                dve.scalar_tensor_tensor(out=G[:, i % 2, :], in0=th, scalar=1.0, in1=G[:, i % 2, :],
                                         op0=ALU.add, op1=ALU.mult).then_inc(gate_ready, 1)

            def softmax_max(b, i):
                dve.wait_ge(s_full, (b * NT + i) + 1)
                dve.tensor_reduce(mx[:, i % 2, 0:1], S[:].rearrange("p n c -> p (n c)"), AX.X, ALU.max).then_inc(max_done, 1)
                dve.wait_ge(max_done, b * NT + i + 1)
                dve.tensor_scalar(mx[:, i % 2, 1:2], mx[:, i % 2, 0:1], -SCALE, None, ALU.mult).then_inc(negmax, 1)

            def pt_units(b, i):
                for n in range(NH):
                    dve.wait_ge(pt_hi, (b * NT + i) * NH + n + 1)
                    sl = slice(n * TH, (n + 1) * TH)
                    split_lo(PT[1][:, sl, :].rearrange("p t c -> p (t c)"), Tp[:, n, :],
                             PT[0][:, sl, :].rearrange("p t c -> p (t c)"), pt_split)

            def finish_tile(b, i):
                dve.wait_ge(p_ready, b * NT + i + 1)
                dve.tensor_scalar(den[:, i % 2, 1:2], den[:, i % 2, 0:1], 2.0, None, ALU.mult).then_inc(den_step, 1)
                dve.wait_ge(den_step, (b * NT + i) * 2 + 1)
                dve.reciprocal(den[:, i % 2, 2:3], den[:, i % 2, 1:2]).then_inc(den_step, 1)
                dve.wait_ge(den_step, (b * NT + i) * 2 + 2)
                dve.wait_ge(gate_ready, b * NT + i + 1)
                dve.wait_ge(o_full, b * NT + i + 1)
                dve.scalar_tensor_tensor(out=G[:, i % 2, :], in0=O[:], scalar=den[:, i % 2, 2:3], in1=G[:, i % 2, :],
                                         op0=ALU.mult, op1=ALU.mult).then_inc(f_done, 1)
                dve.wait_ge(f_done, b * NT + i + 1)
                dve.wait_ge(xres_loaded[i % 2], b * (NT // 2 * 16) + (i // 2 + 1) * 16)
                dve.tensor_tensor(xres[:, i % 2, :], G[:, i % 2, :], xres[:, i % 2, :], ALU.add).then_inc(out_built, 1)

            def body(b, last):
                for u, (kind, n, c) in enumerate(units):
                    r = rank[u]
                    if kind == "h":
                        dve.wait_ge(h_hi, b * H_U + r)
                        split_lo(hs[1][:, (r - 1) % 2, :], h[:, (r - 1) % 2, :], hs[0][:, (r - 1) % 2, :], h_split)
                    elif kind == "y":
                        dve.wait_ge(yv_hi, b * (Y_U + V_U) + r)
                        sl = slice(n * BANK, (n + 1) * BANK)
                        split_lo(yT[1][:, c, sl], unit_bank(u), yT[0][:, c, sl], yv_split)
                    else:
                        dve.wait_ge(yv_hi, b * (Y_U + V_U) + Y_U + r)
                        split_lo(V[1][:, n, :], unit_bank(u), V[0][:, n, :], yv_split)
                    for half in range(NH):
                        if u == last_h[half] + 1:
                            dve.wait_ge(r_full, b * NH + half + 1)
                            dve.tensor_copy(Rs, M[:, half, :]).then_inc(r_copied, 1)
                        if u == last_h[half] + 2:
                            dve.wait_ge(rt_full, b * NH + half + 1)
                            src = (M2[:, :] if half == 0 else M[:, 0, :]).rearrange("p (t r) -> p t r", t=TH)
                            ins = dve.tensor_copy(Z[:, half * TH:(half + 1) * TH, :], src[:, :, 0:2 * LO])
                            ins.then_inc(z_copied, 1)
                    if u == last_h[1] + 3:
                        dve.wait_ge(z_copied, b * NH + 2)
                        routing(b)
                    if u == last_h[1] + 5:
                        routing_pick(b)
                route_tile(b, 0)
                if not last:
                    layernorm_moments(b + 1, 0)
                    layernorm_apply(b * NT + NT, 0)
                gate_tile(b, 0)
                softmax_max(b, 0)
                for i in range(NT):
                    if not last and i + 1 < NT:
                        layernorm_moments(b + 1, i + 1)
                    pt_units(b, i)
                    if i + 1 < NT:
                        route_tile(b, i + 1)
                        if not last:
                            layernorm_apply(b * NT + NT + i + 1, i + 1)
                        gate_tile(b, i + 1)
                        softmax_max(b, i + 1)
                    if not last and i == NT - 2:
                        xt_units(b * XT_U + XT_U, range(0, KC), 0)
                    if not last and i == NT - 1:
                        xt_units(b * XT_U + XT_U, range(KC, XT_U), 1)
                    finish_tile(b, i)

            with dve.Fori(0, B - 1) as b:
                body(b, False)
            body(B - 1, True)

        @block.tensor
        def _(pe):
            def products(dst, chunks, stat, mov, group=None):
                for j, k in enumerate(chunks):
                    for s, (a, m) in enumerate(SPLIT3):
                        mm = pe.matmul(dst, stat(a, k), mov(m, k), start=(j == 0 and s == 0),
                                       stop=(j == len(chunks) - 1 and s == 2))
                return mm

            def xt_unit(n0, v):
                half, k = v // KC, v % KC
                if v >= 3:
                    pe.wait_ge(xt_split, n0 + v - 2)
                for t in range(TH):
                    mm = pe.transpose(xt_bank(v)[:, t * P:(t + 1) * P], xn[:, half * TH + t, k * P:(k + 1) * P], ident[:])
                mm.then_inc(xt_full, 1)

            pe.wait_ge(ident_ready, 2)
            for v in range(XT_U):
                if v % KC == 0:
                    pe.wait_ge(normed, (v // KC + 1) * TH)
                xt_unit(0, v)
            pe.wait_ge(w_loaded[3], 16)
            for v in range(KC):
                for t in range(KC):
                    mm = pe.transpose(unit_bank(v)[:, t * P:(t + 1) * P], wraw[:, 3, t, v * P:(v + 1) * P], ident[:])
                mm.then_inc(pre_full, 1)
            pe.wait_ge(qk_split, 2)
            for v in range(KC):
                pe.wait_ge(pre_split, v + 1)
                products(unit_bank(v), range(KC), lambda a, k: qs[a][:, k, v * P:(v + 1) * P],
                         lambda m, k: ks[m][:, k, :]).then_inc(pre_full, 1)
            pe.wait_ge(pre_split, 2 * KC)
            pe.wait_ge(w1_split, 1)
            pe.wait_ge(w2_split, E + 2)
            pe.wait_ge(table_ready, 1)

            def w2_products(b, r):
                half, c = (r - 1) // HC, (r - 1) % HC
                pe.wait_ge(h_split, b * H_U + r)
                for part in range(2):
                    mm = pe.matmul(M[:, half, :], w2s[:, c, :], hs[part][:, (r - 1) % 2, :],
                                   start=(c == 0 and part == 0), stop=(c == HC - 1 and part == 1))
                if c == HC - 1:
                    mm.then_inc(r_full, 1)

            def turn_router(b, half):
                pe.wait_ge(r_copied, b * NH + half + 1)
                dst = M2[:, :] if half == 0 else M[:, 0, :]
                for t in range(TH):
                    mm = pe.transpose(dst[:, t * P:(t + 1) * P], Rs[:, t * P:(t + 1) * P], ident[:])
                mm.then_inc(rt_full, 1)

            def gather(b, i):
                if i:
                    pe.wait_ge(routed, b * NT + i)
                for n in range(2):
                    mm = pe.matmul(M[:, n, :], onehotT[:, i * P:(i + 1) * P], table[:, n * D:(n + 1) * D],
                                   start=True, stop=True)
                mm.then_inc(gathered, 1)

            def scores(b, i, n):
                mm = products(S[:, n, :], range(KC), lambda a, k: yT[a][:, k, i * P:(i + 1) * P],
                              lambda m, k: xnT[m][:, k, n * BANK:(n + 1) * BANK])
                if n == NH - 1:
                    mm.then_inc(s_full, 1)

            def turn_probs(b, i):
                pe.wait_ge(p_ready, b * NT + i + 1)
                for n in range(NH):
                    if i == NT - 1:
                        pe.wait_ge(pt_split, (b * NT + i - 1) * NH + n + 1)
                    for t in range(TH):
                        c = n * TH + t
                        mm = pe.transpose(Tp[:, n, t * P:(t + 1) * P], Pr[:, c * P:(c + 1) * P], ident[:])
                    mm.then_inc(pt_full, 1)

            def attend(b, i, between):
                for c in range(NT):
                    if c % TH == 0:
                        pe.wait_ge(pt_split, (b * NT + i) * NH + c // TH + 1)
                    for s, (a, m) in enumerate(SPLIT3):
                        mm = pe.matmul(O[:], PT[a][:, c, :], V[m][:, c, :], start=(c == 0 and s == 0),
                                       stop=(c == NT - 1 and s == 2))
                    if c == NT - 1:
                        mm.then_inc(o_full, 1)
                    elif c == TH - 1 and i == NT - 2:
                        mm.then_inc(pv_half, 1)
                    for item in between.get(c, ()):
                        item()

            def body(b, last):
                for u, (kind, n, c) in enumerate(units):
                    if u >= 4:
                        k4, r4 = units[u - 4][0], rank[u - 4]
                        if k4 == "h":
                            pe.wait_ge(h_split, b * H_U + r4)
                        else:
                            pe.wait_ge(yv_split, b * (Y_U + V_U) + r4 + (Y_U if k4 == "v" else 0))
                    if kind == "h":
                        mm = products(unit_bank(u), range(KC), lambda a, k: w1g[a][:, k, c * P:(c + 1) * P],
                                      lambda m, k: xnT[m][:, k, n * BANK:(n + 1) * BANK])
                    elif kind == "y":
                        mm = products(unit_bank(u), range(KC), lambda a, k: A[a][:, k, c * P:(c + 1) * P],
                                      lambda m, k: xnT[m][:, k, n * BANK:(n + 1) * BANK])
                    else:
                        mm = products(unit_bank(u), range(KC), lambda a, k: xnT[a][:, k, n * P:(n + 1) * P],
                                      lambda m, k: WvT[m][:, k, :])
                    mm.then_inc(unit_full, 1)
                    if u and units[u - 1][0] == "h":
                        w2_products(b, rank[u - 1])
                    for half in range(NH):
                        if u == last_h[half] + 2:
                            turn_router(b, half)
                pe.wait_ge(onehot_ready, b + 1)
                for t in range(NT):
                    mm = pe.transpose(Mb[0:EC, t * P:(t + 1) * P], onehot[:, t, :], identb[:])
                mm.then_inc(ot_full, 1)
                pe.wait_ge(yv_split, (b + 1) * (Y_U + V_U))
                scores(b, 0, 0)
                pe.wait_ge(ot_ready, b + 1)
                gather(b, 0)
                scores(b, 0, 1)
                for i in range(NT):
                    if i + 1 < NT:
                        pe.wait_ge(p_ready, b * NT + i + 1)
                        scores(b, i + 1, 0)
                        turn_probs(b, i)
                        gather(b, i + 1)
                        scores(b, i + 1, 1)
                    between = {}
                    if i == NT - 2:
                        between[TH] = [lambda: turn_probs(b, NT - 1)]
                    if not last and i == NT - 2:
                        def first():
                            pe.wait_ge(normed, b * NT + NT + TH)
                            pe.wait_ge(routed, b * NT + NT)
                            xt_unit(b * XT_U + XT_U, 0)
                        between.setdefault(2, []).append(first)
                        for v, c in ((1, 3), (2, 5), (3, 6)):
                            between.setdefault(c, []).append(lambda v=v: xt_unit(b * XT_U + XT_U, v))
                    if not last and i == NT - 1:
                        def second():
                            pe.wait_ge(normed, (b + 2) * NT)
                            xt_unit(b * XT_U + XT_U, KC)
                        between[0] = [second]
                        for v, c in ((5, 2), (6, 4), (7, 6)):
                            between[c] = [lambda v=v: xt_unit(b * XT_U + XT_U, v)]
                    attend(b, i, between)
                if not last:
                    pe.wait_ge(xt_split, (b + 2) * XT_U)

            with pe.Fori(0, B - 1) as b:
                body(b, False)
            body(B - 1, True)


_INS = ["L0_attn_x", "L0_attn_Wq", "L0_attn_Wk", "L0_attn_Wv", "L0_ffn_W1", "L0_ffn_b1", "L0_ffn_W2", "L0_ffn_b2",
        "L0_ffn_Wg1", "L0_ffn_bg1", "L0_ffn_Wg2", "L0_ffn_bg2", "L0_ffn_expert_scales", "L0_ffn_expert_biases"]


def kernel(**inputs):
    import numpy as _np
    import concourse.bacc as _bacc
    from concourse import mybir as _mybir
    from concourse.bass_utils import run_bass_kernel_spmd as _run

    nc = _bacc.Bacc("TRN2", target_bir_lowering=False, num_devices=1)
    arrays, args = {}, []
    for name in _INS:
        a = _np.ascontiguousarray(inputs[name])
        arrays[name] = a
        args.append(nc.dram_tensor(name, a.shape, _mybir.dt.from_np(a.dtype), kind="ExternalInput").ap())
    shape = arrays["L0_attn_x"].shape
    args.append(nc.dram_tensor("out", shape, _mybir.dt.float32, kind="ExternalOutput").ap())
    routed_attention_block(nc, *args)
    r = _run(nc, [arrays], core_ids=[0])
    return r.results[0]["out"]
```

```python
from contextlib import ExitStack

import concourse.bass as bass
from concourse import mybir

F32 = mybir.dt.float32
F32R = mybir.dt.float32r
BF16 = mybir.dt.bfloat16
ALU = mybir.AluOpType
ACT = mybir.ActivationFunctionType
AX = mybir.AxisListType

P = 128
BANK = 512
EPS = 1e-5


def routed_attention_block(nc, x, Wq, Wk, Wv, W1, b1, W2, b2, Wg1, bg1, Wg2, bg2, scales, biases, out):
    B, T, D = x.shape
    RH = W1.shape[1]
    E = W2.shape[1]
    KC = D // P
    NT = T // P
    NH = T // BANK
    TH = NT // NH
    HC = 2 * RH // P
    SCALE = 1.0 / float(D) ** 0.5
    assert D == BANK and T == 2 * BANK and RH == 2 * P and E == 16

    XT_U = KC * NH
    H_U = HC * NH
    Y_U = KC * NH
    V_U = NT
    U = H_U + Y_U + V_U
    LO = 32
    SMALLB = HC + 2
    EC = 3 * 32

    x_t = x.rearrange("b (t p) d -> (b t) p d", p=P)
    out_t = out.rearrange("b (t p) d -> (b t) p d", p=P)

    units = []
    for n in range(NH):
        units += [("h", n, c) for c in range(HC)] + [("y", n, c) for c in range(KC)]
    units += [("v", t, 0) for t in range(NT)]
    rank = []
    for u, (kind, _, _) in enumerate(units):
        rank.append(sum(k == kind for k, _, _ in units[:u + 1]))
    unit_at = [u % 4 for u in range(U - V_U)] + [0, 1, 2, 3, 2, 3, 2, 3]
    FIRST_SCORES = U - 3
    last_h = [max(u for u, (k, n, _) in enumerate(units) if k == "h" and n == half) for half in range(NH)]

    with ExitStack() as ctx:
        def sb(name, shape, dt, where=ctx):
            return where.enter_context(nc.sbuf_tensor(name, shape, dt))

        def sem(name):
            return ctx.enter_context(nc.semaphore(name))

        w1g = [sb(f"w1g_{p}", [P, KC, 2 * RH], F32R) for p in ("hi", "lo")]
        A = [sb(f"A_{p}", [P, KC, D], F32R) for p in ("hi", "lo")]
        WvT = [sb(f"WvT_{p}", [P, KC, D], F32R) for p in ("hi", "lo")]
        xnT = [sb(f"xnT_{p}", [P, KC, T], F32R) for p in ("hi", "lo")]
        PT = [sb(f"PT_{p}", [P, NT, P], F32R) for p in ("hi", "lo")]
        w2s = sb("w2s", [P, HC, P], F32R)
        table = sb("table", [EC, 2 * D], BF16)
        ident = sb("ident", [P, P], F32)
        identb = sb("identb", [P, P], BF16)
        xstage = sb("xstage", [P, 2, D], F32)
        xres = sb("xres", [P, 2, D], F32)
        xn = sb("xn", [P, NT, D], F32)
        Pr = sb("Pr", [P, T], F32)
        G = sb("G", [P, 2, D], F32)
        h = sb("h", [P, 2, BANK], F32)
        th = h[:, 0, :]
        hs = [sb(f"h_{p}", [P, 2, BANK], F32R) for p in ("hi", "lo")]
        Rs = G[:, 1, :]
        Z = G[:, 0, :].rearrange("p (t r) -> p t r", t=NT)
        z = sb("z", [P, NT, E + 1], F32)
        rs = sb("rs", [P, NT, E], F32)
        onehot = sb("onehot", [P, NT, EC], BF16)
        onehotT = sb("onehotT", [EC, T], BF16)
        b2g = sb("b2g", [P, E + 1], F32)
        rev = sb("rev", [P, E], F32)
        bcol = sb("bcol", [P, HC], F32)
        st = sb("st", [P, NT, 6], F32)
        mv = sb("mv", [P, NT, 2], F32)
        rstd = sb("rstd", [P, 2, NT], F32)
        epsc = sb("epsc", [P, 2, TH], F32)
        mx = sb("mx", [P, 2, 2], F32)
        den = sb("den", [P, 2, 3], F32)
        gt = sb("gt", [P, 3, NT], F32)
        sm = sb("sm", [P, 4, NT], F32)

        S = ctx.enter_context(nc.psum_tensor("S", [P, NH, BANK], F32))
        Tp = ctx.enter_context(nc.psum_tensor("Tp", [P, NH, BANK], F32))
        O = ctx.enter_context(nc.psum_tensor("O", [P, BANK], F32))
        M = ctx.enter_context(nc.psum_tensor("M", [P, 2, BANK], F32))
        M2 = ctx.enter_context(nc.psum_tensor("M2", [P, BANK], F32))
        Mb = M2[:].bitcast(BF16)

        def four(n):
            return S[:, n, :] if n < 2 else Tp[:, n - 2, :]

        def xt_bank(v):
            return M[:, v % 2, :]

        def o_bank(i):
            return O[:, :] if i % 2 == 0 else M2[:, :]

        ident_ready = sem("ident_ready")
        consts_set = sem("consts_set")
        w2_loaded = sem("w2_loaded")
        table_loaded = sem("table_loaded")
        bias_loaded = sem("bias_loaded")
        x0_loaded = [sem(f"x0_loaded{i}") for i in range(NH)]
        w_loaded = [sem(f"w_loaded{i}") for i in range(4)]
        w_hi = sem("w_hi")
        w1_split = sem("w1_split")
        wq_split = sem("wq_split")
        w2_split = sem("w2_split")
        w2_zeroed = sem("w2_zeroed")
        table_zeroed = sem("table_zeroed")
        wk_split = sem("wk_split")
        table_step = sem("table_step")
        table_ready = sem("table_ready")
        pre_full = sem("pre_full")
        pre_hi = sem("pre_hi")
        pre_split = sem("pre_split")
        x_loaded = [sem(f"x_loaded{i}") for i in range(2)]
        stats_done = sem("stats_done")
        moments_done = sem("moments_done")
        var_eps = sem("var_eps")
        rstd_done = sem("rstd_done")
        normed = sem("normed")
        xt_full = sem("xt_full")
        xt_hi = sem("xt_hi")
        xt_split = sem("xt_split")
        unit_full = sem("unit_full")
        act_done = sem("act_done")
        h_hi = sem("h_hi")
        h_split = sem("h_split")
        yv_hi = sem("yv_hi")
        yv_split = sem("yv_split")
        r_full = sem("r_full")
        r_copied = sem("r_copied")
        z_copied = sem("z_copied")
        rt_full = sem("rt_full")
        z_ready = sem("z_ready")
        gate_exp = sem("gate_exp")
        route = sem("route")
        route_sub = sem("route_sub")
        route_exp = sem("route_exp")
        onehot_ready = sem("onehot_ready")
        ot_full = sem("ot_full")
        ot_ready = sem("ot_ready")
        gathered = sem("gathered")
        scaled = sem("scaled")
        routed = sem("routed")
        tanh_done = sem("tanh_done")
        gate_ready = sem("gate_ready")
        s_full = sem("s_full")
        max_done = sem("max_done")
        negmax = sem("negmax")
        p_ready = sem("p_ready")
        pt_full = sem("pt_full")
        pt_hi = sem("pt_hi")
        pt_split = sem("pt_split")
        pv_half = sem("pv_half")
        o_full = sem("o_full")
        den_step = sem("den_step")
        f_done = sem("f_done")
        xres_loaded = [sem(f"xres_loaded{i}") for i in range(2)]
        out_built = sem("out_built")
        stored = sem("stored")

        setup = ExitStack()
        wraw = sb("wraw", [P, 4, KC, D], F32, setup)
        qs = [sb(f"Wq_{p}", [P, KC, D], F32R, setup) for p in ("hi", "lo")]
        ks = [sb(f"Wk_{p}", [P, KC, D], F32R, setup) for p in ("hi", "lo")]
        setup.close()
        yT = [sb(f"yT_{p}", [P, KC, T], F32R) for p in ("hi", "lo")]
        V = [sb(f"V_{p}", [P, NT, D], F32R) for p in ("hi", "lo")]
        w2raw = th[:, 0:HC * LO].rearrange("p (c e) -> p c e", c=HC)
        traw = Pr[0:EC, :]

        SPLIT3 = ((0, 0), (0, 1), (1, 0))

        block = ctx.enter_context(nc.Block())

        @block.sync
        def _(sp):
            def load_stage(t, slot, free):
                sp.wait_ge(normed, free)
                sp.dma_start(xstage[:, slot, :], x_t[t] if isinstance(t, int) else
                             x_t[bass.ds(t, 1)].rearrange("a p d -> p (a d)")).then_inc(x_loaded[slot], 16)

            def load_res(t, slot):
                sp.dma_start(xres[:, slot, :], x_t[t] if isinstance(t, int) else
                             x_t[bass.ds(t, 1)].rearrange("a p d -> p (a d)")).then_inc(xres_loaded[slot], 16)

            def load_half(n):
                sp.dma_start(xn[:, n * TH:(n + 1) * TH, :],
                             x_t[n * TH:(n + 1) * TH].rearrange("t p d -> p t d")).then_inc(x0_loaded[n], 16)

            def load_w(i, src, dst):
                sp.dma_start(dst, src.rearrange("(k p) d -> p k d", p=P)).then_inc(w_loaded[i], 16)

            load_half(0)
            load_w(1, Wq, wraw[:, 1])
            load_w(2, Wk, wraw[:, 2])
            load_half(1)
            load_w(3, Wv, wraw[:, 3])
            sp.wait_ge(w2_zeroed, 1)
            for c in range(HC // 2):
                sp.dma_start(w2raw[:, c, 0:E], W2[c * P:(c + 1) * P, :]).then_inc(w2_loaded, 16)
                sp.dma_start(w2raw[:, HC // 2 + c, E:E + 1], Wg2[c * P:(c + 1) * P, :]).then_inc(w2_loaded, 16)
            for c in range(HC // 2):
                col = slice(c * P, (c + 1) * P)
                sp.dma_start(bcol[:, c:c + 1], b1[col].rearrange("(p o) -> p o", o=1)).then_inc(bias_loaded, 16)
                sp.dma_start(bcol[:, HC // 2 + c:HC // 2 + c + 1],
                             bg1[col].rearrange("(p o) -> p o", o=1)).then_inc(bias_loaded, 16)
            sp.dma_start(b2g[:, 0:E], b2.partition_broadcast(P)).then_inc(bias_loaded, 16)
            sp.dma_start(b2g[:, E:E + 1], bg2.partition_broadcast(P)).then_inc(bias_loaded, 16)
            sp.wait_ge(table_zeroed, 1)
            for part in range(3):
                sp.dma_start(traw[32 * part:32 * part + E, 0:D], scales).then_inc(table_loaded, 16)
                sp.dma_start(traw[32 * part:32 * part + E, D:], biases).then_inc(table_loaded, 16)
            for t in range(2):
                load_res(t, t)

            def body(b, last):
                if not last:
                    load_stage(b * NT + NT, 0, b * NT + NT - 1)
                    load_stage(b * NT + NT + 1, 1, b * NT + NT)
                for i in range(NT):
                    if not last and i + 2 < NT:
                        load_stage(b * NT + NT + i + 2, i % 2, b * NT + NT + i + 1)
                    sp.wait_ge(out_built, b * NT + i + 1)
                    sp.dma_start(out_t[b * NT + i] if isinstance(b, int) else
                                 out_t[bass.ds(b * NT + i, 1)].rearrange("a p d -> p (a d)"),
                                 xres[:, i % 2, :]).then_inc(stored, 16)
                    if not (last and i >= NT - 2):
                        sp.wait_ge(stored, (b * NT + i + 1) * 16)
                        load_res(b * NT + i + 2, i % 2)

            with sp.Fori(0, B - 1) as b:
                body(b, False)
            body(B - 1, True)
            sp.wait_ge(stored, B * NT * 16)

        @block.gpsimd
        def _(pool):
            pool.memset(ident[:], 0.0).then_inc(consts_set, 1)
            pool.wait_ge(consts_set, 1)
            pool.affine_select(out=ident[:], in_=ident[:], compare_op=ALU.not_equal, fill=1.0, base=0,
                               pattern=[[-1, P]], channel_multiplier=1).then_inc(ident_ready, 1)
            pool.memset(epsc[:, 0, :], EPS)
            pool.memset(epsc[:, 1, :], -0.5).then_inc(consts_set, 1)
            pool.wait_ge(consts_set, 2)
            pool.wait_ge(ident_ready, 1)
            pool.tensor_copy(identb[:], ident[:]).then_inc(ident_ready, 1)
            pool.memset(traw, 0.0).then_inc(table_zeroed, 1)

            def invert_std(moments, n, tiles):
                pool.wait_ge(moments_done, moments)
                k = tiles.stop - tiles.start
                pool.tensor_tensor(rstd[:, 0, tiles], mv[:, tiles, 1], epsc[:, 0, 0:k], ALU.add).then_inc(var_eps, 1)
                pool.wait_ge(var_eps, n + 1)
                pool.tensor_tensor(rstd[:, 1, tiles], rstd[:, 0, tiles], epsc[:, 1, 0:k], ALU.pow).then_inc(rstd_done, 1)

            invert_std(TH, 0, slice(0, TH))
            pool.wait_ge(w_hi, 1)
            pool.tensor_tensor(qs[1][:], wraw[:, 1], qs[0][:].bitcast(F32), ALU.subtract).then_inc(wq_split, 1)
            invert_std(NT, 1, slice(TH, NT))
            pool.wait_ge(table_loaded, 16 * 6)
            pool.wait_ge(rstd_done, 2)
            steps = 0

            def step(ins):
                nonlocal steps
                ins.then_inc(table_step, 1)
                steps += 1
                pool.wait_ge(table_step, steps)

            step(pool.tensor_copy(table[:], traw))
            for part in (1, 2):
                for r in range(32 * part, EC, 32):
                    step(pool.tensor_tensor(traw[r:r + 32], traw[r:r + 32], table[r:r + 32, :], ALU.subtract))
                    step(pool.tensor_copy(table[r:r + 32, :], traw[r:r + 32]))
            pool.memset(epsc[:, 0, :], EPS).then_inc(table_ready, 1)

            def body(b):
                for i in range(NT):
                    n = b * NT + NT + i
                    invert_std(n + 1, b * NT + NH + i, slice(i, i + 1))

            with pool.Fori(0, B - 1) as b:
                body(b)

        @block.scalar
        def _(act):
            for src, cols in ((W1, slice(0, RH)), (Wg1, slice(RH, 2 * RH))):
                act.dma_start(wraw[:, 0, :, cols], src.rearrange("(k p) d -> p k d", p=P)).then_inc(w_loaded[0], 16)

            def split_hi(dst, src, done):
                act.activation(dst, src, ACT.Copy).then_inc(done, 1)

            for i, part, need in ((1, qs, 16), (2, ks, 16), (0, w1g, 32)):
                act.wait_ge(w_loaded[i], need)
                split_hi(part[0][:], wraw[:, i], w_hi)

            def xt_units(n0, lot, half):
                for v in lot:
                    act.wait_ge(xt_full, n0 + v + 1)
                    split_hi(xnT[0][:, v % KC, half * BANK:half * BANK + BANK], xt_bank(v), xt_hi)

            xt_units(0, range(0, KC), 0)
            xt_units(0, range(KC, XT_U), 1)
            for v in range(2 * KC):
                act.wait_ge(pre_full, v + 1)
                split_hi((WvT if v < KC else A)[0][:, v % KC, :], four(v % 4), pre_hi)
            act.wait_ge(bias_loaded, 16 * SMALLB)

            def softmax_exp(b, i):
                act.wait_ge(negmax, b * NT + i + 1)
                act.activation(Pr[:], S[:].rearrange("p n c -> p (n c)"), ACT.Exp, bias=mx[:, i % 2, 1:2],
                               scale=SCALE, accum_out=den[:, i % 2, 0:1]).then_inc(p_ready, 1)

            def gate_tanh(b, i):
                act.wait_ge(routed, b * NT + i + 1)
                act.activation(th, G[:, i % 2, :], ACT.Tanh, scale=0.5).then_inc(tanh_done, 1)

            def pt_unit(b, i, n):
                act.wait_ge(pt_full, (b * NT + i) * NH + n + 1)
                if i == NT - 1:
                    if n == 0:
                        act.wait_ge(pv_half, b + 1)
                    else:
                        act.wait_ge(o_full, b * NT + NT - 1)
                split_hi(PT[0][:, n * TH:(n + 1) * TH, :].rearrange("p t c -> p (t c)"), Tp[:, n, :], pt_hi)

            def body(b, last):
                for u, (kind, n, c) in enumerate(units):
                    act.wait_ge(unit_full, b * U + u + 1)
                    if kind == "h":
                        r = rank[u]
                        if r > 2:
                            act.wait_ge(h_split, b * H_U + r - 2)
                        act.activation(h[:, (r - 1) % 2, :], four(unit_at[u]), ACT.Relu if c < HC // 2 else ACT.Tanh,
                                       bias=bcol[:, c:c + 1]).then_inc(act_done, 1)
                        act.wait_ge(act_done, b * H_U + r)
                        split_hi(hs[0][:, (r - 1) % 2, :], h[:, (r - 1) % 2, :], h_hi)
                    elif kind == "y":
                        split_hi(yT[0][:, c, n * BANK:(n + 1) * BANK], four(unit_at[u]), yv_hi)
                    else:
                        split_hi(V[0][:, n, :], four(unit_at[u]), yv_hi)
                    if u == last_h[1] + 3:
                        act.wait_ge(z_ready, b + 1)
                        act.activation(gt[:, 0, :], z[:, :, E], ACT.Exp, scale=-1.0).then_inc(gate_exp, 1)
                    if u == last_h[1] + 5:
                        act.wait_ge(route_sub, b + 1)
                        act.activation(rs[:], rs[:], ACT.Exp).then_inc(route_exp, 1)
                    if u == FIRST_SCORES:
                        act.wait_ge(ot_full, b + 1)
                        act.activation(onehotT[:], Mb[0:EC, :], ACT.Copy).then_inc(ot_ready, 1)
                        gate_tanh(b, 0)
                        softmax_exp(b, 0)
                xt0 = b * XT_U + XT_U
                for i in range(NT):
                    if i < NT - 1:
                        pt_unit(b, i, 0)
                        pt_unit(b, i, 1)
                        gate_tanh(b, i + 1)
                        softmax_exp(b, i + 1)
                    else:
                        if not last:
                            xt_units(xt0, range(0, 2), 0)
                        pt_unit(b, i, 0)
                        if not last:
                            xt_units(xt0, range(2, KC), 0)
                        pt_unit(b, i, 1)
                        if not last:
                            xt_units(xt0, range(KC, XT_U), 1)

            with act.Fori(0, B - 1) as b:
                body(b, False)
            body(B - 1, True)

        @block.vector
        def _(dve):
            def layernorm_moments(n, src, t):
                dve.bn_stats(st[:, t, :], src).then_inc(stats_done, 1)
                dve.wait_ge(stats_done, n + 1)
                dve.memset(sm[:, 3, 0:1], 0.0)
                dve.bn_aggr(mv[:, t, :], st[:, t, :]).then_inc(moments_done, 1)

            def layernorm_apply(src, t):
                dve.tensor_scalar(xn[:, t, :], src, mv[:, t, 0:1], rstd[:, 1, t:t + 1],
                                  ALU.subtract, ALU.mult).then_inc(normed, 1)

            def next_moments(b, t):
                dve.wait_ge(x_loaded[t % 2], b * (NT // 2 * 16) + (t // 2 + 1) * 16)
                layernorm_moments(b * NT + NT + t, xstage[:, t % 2, :], t)

            def next_apply(b, t):
                dve.wait_ge(rstd_done, b * NT + NH + t + 1)
                layernorm_apply(xstage[:, t % 2, :], t)

            def split_lo(dst, src, hi, done):
                dve.tensor_tensor(dst, src, hi.bitcast(F32), ALU.subtract).then_inc(done, 1)

            def xt_units(n0, lot, half):
                for v in lot:
                    dve.wait_ge(xt_hi, n0 + v + 1)
                    sl = slice(half * BANK, half * BANK + BANK)
                    split_lo(xnT[1][:, v % KC, sl], xt_bank(v), xnT[0][:, v % KC, sl], xt_split)

            dve.memset(w2raw, 0.0).then_inc(w2_zeroed, 1)
            for e in range(E):
                dve.memset(rev[:, e:e + 1], float(E - e))
            dve.memset(onehot[:], 0.0)
            dve.memset(w2s[:].bitcast(F32), 0.0).then_inc(w2_split, 1)

            def first_moments(half):
                dve.wait_ge(x0_loaded[half], 16)
                for t in range(half * TH, (half + 1) * TH):
                    dve.bn_stats(st[:, t, :], xn[:, t, :]).then_inc(stats_done, 1)
                dve.wait_ge(stats_done, (half + 1) * TH)
                dve.memset(sm[:, 3, 0:1], 0.0)
                for t in range(half * TH, (half + 1) * TH):
                    dve.bn_aggr(mv[:, t, :], st[:, t, :]).then_inc(moments_done, 1)

            def first_apply(half):
                dve.wait_ge(rstd_done, half + 1)
                for t in range(half * TH, (half + 1) * TH):
                    layernorm_apply(xn[:, t, :], t)

            first_moments(0)
            first_apply(0)
            dve.wait_ge(w_hi, 2)
            split_lo(ks[1][:], wraw[:, 2], ks[0][:], wk_split)
            xt_units(0, range(0, KC), 0)
            dve.wait_ge(w_hi, 3)
            split_lo(w1g[1][:], wraw[:, 0], w1g[0][:], w1_split)
            first_moments(1)
            first_apply(1)
            xt_units(0, range(KC, XT_U), 1)
            dve.wait_ge(w2_loaded, 16 * HC)
            dve.wait_ge(w2_split, 1)
            dve.tensor_copy(w2s[:, :, 0:LO], w2raw).then_inc(w2_split, 1)
            dve.wait_ge(w2_split, 2)
            split_lo(w2s[:, :, LO:2 * LO], w2raw, w2s[:, :, 0:LO], w2_split)
            for v in range(2 * KC):
                dve.wait_ge(pre_hi, v + 1)
                W = WvT if v < KC else A
                split_lo(W[1][:, v % KC, :], four(v % 4), W[0][:, v % KC, :], pre_split)
            dve.wait_ge(bias_loaded, 16 * SMALLB)

            def routing(b):
                STEPS = 12
                done = [b * STEPS]

                def step(ins, sem_=None):
                    ins.then_inc(route, 1)
                    done[0] = done[0] + 1
                    dve.wait_ge(route, done[0])

                def over_tiles(row):
                    return row.unsqueeze(2).to_broadcast([P, NT, E])

                step(dve.tensor_tensor(z[:], Z[:, :, 0:E + 1], Z[:, :, LO:LO + E + 1], ALU.add))
                dve.tensor_tensor(z[:], z[:], b2g[:].unsqueeze(1).to_broadcast([P, NT, E + 1]),
                                  ALU.add).then_inc(z_ready, 1)
                dve.wait_ge(gate_exp, b + 1)
                step(dve.tensor_scalar(gt[:, 1, :], gt[:, 0, :], 1.0, None, ALU.add))
                step(dve.reciprocal(gt[:, 2, :], gt[:, 1, :]))
                step(dve.tensor_tensor(rs[:], z[:, :, 0:E], over_tiles(gt[:, 2, :]), ALU.mult))
                step(dve.tensor_reduce(sm[:, 0, :], rs[:], AX.X, ALU.max))
                dve.tensor_tensor(rs[:], rs[:], over_tiles(sm[:, 0, :]), ALU.subtract).then_inc(route_sub, 1)

            def routing_pick(b):
                STEPS = 12
                done = [b * STEPS + 5]

                def step(ins):
                    ins.then_inc(route, 1)
                    done[0] = done[0] + 1
                    dve.wait_ge(route, done[0])

                def over_tiles(row):
                    return row.unsqueeze(2).to_broadcast([P, NT, E])

                dve.wait_ge(route_exp, b + 1)
                step(dve.tensor_reduce(sm[:, 1, :], rs[:], AX.X, ALU.add))
                step(dve.reciprocal(sm[:, 2, :], sm[:, 1, :]))
                step(dve.tensor_tensor(rs[:], rs[:], over_tiles(sm[:, 2, :]), ALU.mult))
                step(dve.tensor_reduce(sm[:, 0, :], rs[:], AX.X, ALU.max))
                step(dve.tensor_tensor(rs[:], rs[:], over_tiles(sm[:, 0, :]), ALU.is_ge))
                step(dve.tensor_tensor(rs[:], rs[:], rev[:].unsqueeze(1).to_broadcast([P, NT, E]), ALU.mult))
                step(dve.tensor_reduce(sm[:, 1, :], rs[:], AX.X, ALU.max))
                for part in range(3):
                    ins = dve.tensor_tensor(onehot[:, :, 32 * part:32 * part + E], rs[:], over_tiles(sm[:, 1, :]), ALU.is_equal)
                ins.then_inc(onehot_ready, 1)

            def route_tile(b, i):
                dve.wait_ge(gathered, b * NT + i + 1)
                if i >= 2:
                    dve.wait_ge(out_built, b * NT + i - 1)
                dve.tensor_tensor(G[:, i % 2, :], M[:, 0, :], xn[:, i, :], ALU.mult).then_inc(scaled, 1)
                dve.wait_ge(scaled, b * NT + i + 1)
                dve.tensor_tensor(G[:, i % 2, :], G[:, i % 2, :], M[:, 1, :], ALU.add).then_inc(routed, 1)

            def gate_tile(b, i):
                dve.wait_ge(tanh_done, b * NT + i + 1)
                dve.scalar_tensor_tensor(out=G[:, i % 2, :], in0=th, scalar=1.0, in1=G[:, i % 2, :],
                                         op0=ALU.add, op1=ALU.mult).then_inc(gate_ready, 1)

            def softmax_max(b, i):
                dve.wait_ge(s_full, (b * NT + i) + 1)
                dve.tensor_reduce(mx[:, i % 2, 0:1], S[:].rearrange("p n c -> p (n c)"), AX.X, ALU.max).then_inc(max_done, 1)
                dve.wait_ge(max_done, b * NT + i + 1)
                dve.tensor_scalar(mx[:, i % 2, 1:2], mx[:, i % 2, 0:1], -SCALE, None, ALU.mult).then_inc(negmax, 1)

            def pt_unit(b, i, n):
                dve.wait_ge(pt_hi, (b * NT + i) * NH + n + 1)
                sl = slice(n * TH, (n + 1) * TH)
                split_lo(PT[1][:, sl, :].rearrange("p t c -> p (t c)"), Tp[:, n, :],
                         PT[0][:, sl, :].rearrange("p t c -> p (t c)"), pt_split)

            def finish_tile(b, i):
                dve.wait_ge(p_ready, b * NT + i + 1)
                dve.tensor_scalar(den[:, i % 2, 1:2], den[:, i % 2, 0:1], 2.0, None, ALU.mult).then_inc(den_step, 1)
                dve.wait_ge(den_step, (b * NT + i) * 2 + 1)
                dve.reciprocal(den[:, i % 2, 2:3], den[:, i % 2, 1:2]).then_inc(den_step, 1)
                dve.wait_ge(den_step, (b * NT + i) * 2 + 2)
                dve.wait_ge(gate_ready, b * NT + i + 1)
                dve.wait_ge(o_full, b * NT + i + 1)
                dve.scalar_tensor_tensor(out=G[:, i % 2, :], in0=o_bank(i), scalar=den[:, i % 2, 2:3], in1=G[:, i % 2, :],
                                         op0=ALU.mult, op1=ALU.mult).then_inc(f_done, 1)
                dve.wait_ge(f_done, b * NT + i + 1)
                dve.wait_ge(xres_loaded[i % 2], b * (NT // 2 * 16) + (i // 2 + 1) * 16)
                dve.tensor_tensor(xres[:, i % 2, :], G[:, i % 2, :], xres[:, i % 2, :], ALU.add).then_inc(out_built, 1)

            def body(b, last):
                for u, (kind, n, c) in enumerate(units):
                    r = rank[u]
                    if kind == "h":
                        dve.wait_ge(h_hi, b * H_U + r)
                        split_lo(hs[1][:, (r - 1) % 2, :], h[:, (r - 1) % 2, :], hs[0][:, (r - 1) % 2, :], h_split)
                    elif kind == "y":
                        dve.wait_ge(yv_hi, b * (Y_U + V_U) + r)
                        sl = slice(n * BANK, (n + 1) * BANK)
                        split_lo(yT[1][:, c, sl], four(unit_at[u]), yT[0][:, c, sl], yv_split)
                    else:
                        dve.wait_ge(yv_hi, b * (Y_U + V_U) + Y_U + r)
                        split_lo(V[1][:, n, :], four(unit_at[u]), V[0][:, n, :], yv_split)
                    for half in range(NH):
                        if u == last_h[half] + 1:
                            dve.wait_ge(r_full, b * NH + half + 1)
                            dve.tensor_copy(Rs, M[:, half, :]).then_inc(r_copied, 1)
                        if u == last_h[half] + 2:
                            dve.wait_ge(rt_full, b * NH + half + 1)
                            src = (M2[:, :] if half == 0 else M[:, 0, :]).rearrange("p (t r) -> p t r", t=TH)
                            ins = dve.tensor_copy(Z[:, half * TH:(half + 1) * TH, :], src[:, :, 0:2 * LO])
                            ins.then_inc(z_copied, 1)
                    if u == last_h[1] + 3:
                        dve.wait_ge(z_copied, b * NH + 2)
                        routing(b)
                    if u == last_h[1] + 5:
                        routing_pick(b)
                    if u == FIRST_SCORES:
                        route_tile(b, 0)
                        if not last:
                            next_moments(b, 0)
                        gate_tile(b, 0)
                        softmax_max(b, 0)
                        if not last:
                            next_apply(b, 0)
                xt0 = b * XT_U + XT_U
                for i in range(NT):
                    if i < NT - 1:
                        if not last:
                            next_moments(b, i + 1)
                        pt_unit(b, i, 0)
                        pt_unit(b, i, 1)
                        route_tile(b, i + 1)
                        if not last:
                            next_apply(b, i + 1)
                        gate_tile(b, i + 1)
                        softmax_max(b, i + 1)
                        if i < NT - 2:
                            finish_tile(b, i)
                    else:
                        if not last:
                            xt_units(xt0, range(0, 2), 0)
                        pt_unit(b, i, 0)
                        if not last:
                            xt_units(xt0, range(2, KC), 0)
                        pt_unit(b, i, 1)
                        finish_tile(b, i - 1)
                        if not last:
                            xt_units(xt0, range(KC, XT_U), 1)
                        finish_tile(b, i)

            with dve.Fori(0, B - 1) as b:
                body(b, False)
            body(B - 1, True)

        @block.tensor
        def _(pe):
            def products(dst, chunks, stat, mov, group=None):
                for j, k in enumerate(chunks):
                    for s, (a, m) in enumerate(SPLIT3):
                        mm = pe.matmul(dst, stat(a, k), mov(m, k), start=(j == 0 and s == 0),
                                       stop=(j == len(chunks) - 1 and s == 2))
                return mm

            def xt_unit(n0, v):
                half, k = v // KC, v % KC
                if v >= 2:
                    pe.wait_ge(xt_split, n0 + v - 1)
                for t in range(TH):
                    mm = pe.transpose(xt_bank(v)[:, t * P:(t + 1) * P], xn[:, half * TH + t, k * P:(k + 1) * P], ident[:])
                mm.then_inc(xt_full, 1)

            pe.wait_ge(ident_ready, 2)
            for v in range(XT_U):
                if v % KC == 0:
                    pe.wait_ge(normed, (v // KC + 1) * TH)
                xt_unit(0, v)
            pe.wait_ge(w_loaded[3], 16)
            for v in range(KC):
                for t in range(KC):
                    mm = pe.transpose(four(v % 4)[:, t * P:(t + 1) * P], wraw[:, 3, t, v * P:(v + 1) * P], ident[:])
                mm.then_inc(pre_full, 1)
            pe.wait_ge(wq_split, 1)
            pe.wait_ge(wk_split, 1)
            for v in range(KC):
                pe.wait_ge(pre_split, v + 1)
                products(four(v % 4), range(KC), lambda a, k: qs[a][:, k, v * P:(v + 1) * P],
                         lambda m, k: ks[m][:, k, :]).then_inc(pre_full, 1)
            pe.wait_ge(pre_split, 2 * KC)
            pe.wait_ge(w1_split, 1)
            pe.wait_ge(w2_split, 3)

            def w2_products(b, r):
                half, c = (r - 1) // HC, (r - 1) % HC
                pe.wait_ge(h_split, b * H_U + r)
                for part in range(2):
                    mm = pe.matmul(M[:, half, :], w2s[:, c, :], hs[part][:, (r - 1) % 2, :],
                                   start=(c == 0 and part == 0), stop=(c == HC - 1 and part == 1))
                if c == HC - 1:
                    mm.then_inc(r_full, 1)

            def turn_router(b, half):
                pe.wait_ge(r_copied, b * NH + half + 1)
                dst = M2[:, :] if half == 0 else M[:, 0, :]
                for t in range(TH):
                    mm = pe.transpose(dst[:, t * P:(t + 1) * P], Rs[:, t * P:(t + 1) * P], ident[:])
                mm.then_inc(rt_full, 1)

            def gather(b, i):
                if i:
                    pe.wait_ge(routed, b * NT + i)
                else:
                    pe.wait_ge(table_ready, 1)
                for n in range(2):
                    mm = pe.matmul(M[:, n, :], onehotT[:, i * P:(i + 1) * P], table[:, n * D:(n + 1) * D],
                                   start=True, stop=True)
                mm.then_inc(gathered, 1)

            def scores(b, i, n):
                mm = products(S[:, n, :], range(KC), lambda a, k: yT[a][:, k, i * P:(i + 1) * P],
                              lambda m, k: xnT[m][:, k, n * BANK:(n + 1) * BANK])
                if n == NH - 1:
                    mm.then_inc(s_full, 1)

            def turn_probs(b, i):
                pe.wait_ge(p_ready, b * NT + i + 1)
                for n in range(NH):
                    if i == NT - 1:
                        pe.wait_ge(pt_split, (b * NT + i - 1) * NH + n + 1)
                    for t in range(TH):
                        c = n * TH + t
                        mm = pe.transpose(Tp[:, n, t * P:(t + 1) * P], Pr[:, c * P:(c + 1) * P], ident[:])
                    mm.then_inc(pt_full, 1)

            def attend(b, i, between):
                for c in range(NT):
                    if c % TH == 0:
                        pe.wait_ge(pt_split, (b * NT + i) * NH + c // TH + 1)
                    for s, (a, m) in enumerate(SPLIT3):
                        mm = pe.matmul(o_bank(i), PT[a][:, c, :], V[m][:, c, :], start=(c == 0 and s == 0),
                                       stop=(c == NT - 1 and s == 2))
                    if c == NT - 1:
                        mm.then_inc(o_full, 1)
                    elif c == TH - 1 and i == NT - 2:
                        mm.then_inc(pv_half, 1)
                    for item in between.get(c, ()):
                        item()

            def body(b, last):
                def unit_read(u):
                    kind, r = units[u][0], rank[u]
                    if kind == "h":
                        pe.wait_ge(h_split, b * H_U + r)
                    else:
                        pe.wait_ge(yv_split, b * (Y_U + V_U) + r + (Y_U if kind == "v" else 0))

                for u, (kind, n, c) in enumerate(units):
                    if u == 0:
                        pe.wait_ge(xt_split, b * XT_U + KC)
                    if u == HC + KC:
                        pe.wait_ge(xt_split, b * XT_U + XT_U)
                    before = [w for w in range(u) if unit_at[w] == unit_at[u]]
                    if before:
                        unit_read(before[-1])
                    if kind == "h":
                        mm = products(four(unit_at[u]), range(KC), lambda a, k: w1g[a][:, k, c * P:(c + 1) * P],
                                      lambda m, k: xnT[m][:, k, n * BANK:(n + 1) * BANK])
                    elif kind == "y":
                        mm = products(four(unit_at[u]), range(KC), lambda a, k: A[a][:, k, c * P:(c + 1) * P],
                                      lambda m, k: xnT[m][:, k, n * BANK:(n + 1) * BANK])
                    else:
                        mm = products(four(unit_at[u]), range(KC), lambda a, k: xnT[a][:, k, n * P:(n + 1) * P],
                                      lambda m, k: WvT[m][:, k, :])
                    mm.then_inc(unit_full, 1)
                    if u and units[u - 1][0] == "h":
                        w2_products(b, rank[u - 1])
                    for half in range(NH):
                        if u == last_h[half] + 2:
                            turn_router(b, half)
                    if u == FIRST_SCORES:
                        pe.wait_ge(onehot_ready, b + 1)
                        for t in range(NT):
                            mm = pe.transpose(Mb[0:EC, t * P:(t + 1) * P], onehot[:, t, :], identb[:])
                        mm.then_inc(ot_full, 1)
                        unit_read(U - V_U)
                        scores(b, 0, 0)
                        pe.wait_ge(ot_ready, b + 1)
                        gather(b, 0)
                        unit_read(U - V_U + 1)
                        scores(b, 0, 1)
                for i in range(NT):
                    if i + 1 < NT:
                        pe.wait_ge(p_ready, b * NT + i + 1)
                        scores(b, i + 1, 0)
                        if i == 0:
                            unit_read(U - 1)
                        turn_probs(b, i)
                        gather(b, i + 1)
                        scores(b, i + 1, 1)
                    between = {}
                    xt0 = b * XT_U + XT_U
                    if i == NT - 2:
                        between[TH] = [lambda: turn_probs(b, NT - 1)]
                        if not last:
                            pe.wait_ge(normed, b * NT + NT + TH)
                            pe.wait_ge(routed, b * NT + NT)
                            for v, c in enumerate((2, 3, 5, 6)):
                                between.setdefault(c, []).append(lambda v=v: xt_unit(xt0, v))
                    if not last and i == NT - 1:
                        pe.wait_ge(normed, b * NT + 2 * NT)
                        for v, c in enumerate((1, 3, 5, 6)):
                            between[c] = [lambda v=v: xt_unit(xt0, KC + v)]
                    attend(b, i, between)

            with pe.Fori(0, B - 1) as b:
                body(b, False)
            body(B - 1, True)


_INS = ["L0_attn_x", "L0_attn_Wq", "L0_attn_Wk", "L0_attn_Wv", "L0_ffn_W1", "L0_ffn_b1", "L0_ffn_W2", "L0_ffn_b2",
        "L0_ffn_Wg1", "L0_ffn_bg1", "L0_ffn_Wg2", "L0_ffn_bg2", "L0_ffn_expert_scales", "L0_ffn_expert_biases"]


def kernel(**inputs):
    import numpy as _np
    import concourse.bacc as _bacc
    from concourse import mybir as _mybir
    from concourse.bass_utils import run_bass_kernel_spmd as _run

    nc = _bacc.Bacc("TRN2", target_bir_lowering=False, num_devices=1)
    arrays, args = {}, []
    for name in _INS:
        a = _np.ascontiguousarray(inputs[name])
        arrays[name] = a
        args.append(nc.dram_tensor(name, a.shape, _mybir.dt.from_np(a.dtype), kind="ExternalInput").ap())
    shape = arrays["L0_attn_x"].shape
    args.append(nc.dram_tensor("out", shape, _mybir.dt.float32, kind="ExternalOutput").ap())
    routed_attention_block(nc, *args)
    r = _run(nc, [arrays], core_ids=[0])
    return r.results[0]["out"]
```

```python
from contextlib import ExitStack

import concourse.bass as bass
from concourse import mybir

F32 = mybir.dt.float32
F32R = mybir.dt.float32r
BF16 = mybir.dt.bfloat16
ALU = mybir.AluOpType
ACT = mybir.ActivationFunctionType
AX = mybir.AxisListType

P = 128
BANK = 512
EPS = 1e-5


def routed_attention_block(nc, x, Wq, Wk, Wv, W1, b1, W2, b2, Wg1, bg1, Wg2, bg2, scales, biases, out):
    B, T, D = x.shape
    RH = W1.shape[1]
    E = W2.shape[1]
    KC = D // P
    NT = T // P
    NH = T // BANK
    TH = NT // NH
    HC = 2 * RH // P
    SCALE = 1.0 / float(D) ** 0.5
    assert D == BANK and T == 2 * BANK and RH == 2 * P and E == 16

    XT_U = KC * NH
    H_U = HC * NH
    Y_U = KC * NH
    V_U = NT
    U = H_U + Y_U + V_U
    LO = 32
    EC = 3 * 32

    x_t = x.rearrange("b (t p) d -> (b t) p d", p=P)
    out_t = out.rearrange("b (t p) d -> (b t) p d", p=P)

    units = []
    for n in range(NH):
        units += [("h", n, c) for c in range(HC)] + [("y", n, c) for c in range(KC)]
    units += [("v", t, 0) for t in range(NT)]
    rank = []
    for u, (kind, _, _) in enumerate(units):
        rank.append(sum(k == kind for k, _, _ in units[:u + 1]))
    unit_at = [u % 4 for u in range(U - V_U)] + [0, 1, 2, 3, 2, 3, 2, 3]
    FIRST_SCORES = U - 3
    last_h = [max(u for u, (k, n, _) in enumerate(units) if k == "h" and n == half) for half in range(NH)]

    with ExitStack() as ctx:
        def sb(name, shape, dt, where=ctx):
            return where.enter_context(nc.sbuf_tensor(name, shape, dt))

        def sem(name):
            return ctx.enter_context(nc.semaphore(name))

        w1g = [sb(f"w1g_{p}", [P, KC, 2 * RH], F32R) for p in ("hi", "lo")]
        A = [sb(f"A_{p}", [P, KC, D], F32R) for p in ("hi", "lo")]
        WvT = [sb(f"WvT_{p}", [P, KC, D], F32R) for p in ("hi", "lo")]
        xnT = [sb(f"xnT_{p}", [P, KC, T], F32R) for p in ("hi", "lo")]
        PT = [sb(f"PT_{p}", [P, NT, P], F32R) for p in ("hi", "lo")]
        w2s = sb("w2s", [P, HC, P], F32R)
        table = sb("table", [EC, 2 * D], BF16)
        ident = sb("ident", [P, P], F32)
        identb = sb("identb", [P, P], BF16)
        xstage = sb("xstage", [P, 2, D], F32)
        xres = sb("xres", [P, 2, D], F32)
        xn = sb("xn", [P, NT, D], F32)
        Pr = sb("Pr", [P, T], F32)
        G = sb("G", [P, 2, D], F32)
        h = sb("h", [P, 2, BANK], F32)
        th = h[:, 0, :]
        hs = [sb(f"h_{p}", [P, 2, BANK], F32R) for p in ("hi", "lo")]
        Rs = G[:, 1, :]
        Z = G[:, 0, :].rearrange("p (t r) -> p t r", t=NT)
        z = sb("z", [P, NT, E + 1], F32)
        rs = sb("rs", [P, NT, E], F32)
        onehot = sb("onehot", [P, NT, EC], BF16)
        onehotT = sb("onehotT", [EC, T], BF16)
        b2g = sb("b2g", [P, E + 1], F32)
        rev = sb("rev", [P, E], F32)
        bcol = sb("bcol", [P, HC], F32)
        st = sb("st", [P, NT, 6], F32)
        mv = sb("mv", [P, NT, 2], F32)
        rstd = sb("rstd", [P, 2, NT], F32)
        epsc = sb("epsc", [P, 2, TH], F32)
        mx = sb("mx", [P, 2, 2], F32)
        den = sb("den", [P, 2, 3], F32)
        gt = sb("gt", [P, 3, NT], F32)
        sm = sb("sm", [P, 4, NT], F32)

        S = ctx.enter_context(nc.psum_tensor("S", [P, NH, BANK], F32))
        Tp = ctx.enter_context(nc.psum_tensor("Tp", [P, NH, BANK], F32))
        O = ctx.enter_context(nc.psum_tensor("O", [P, BANK], F32))
        M = ctx.enter_context(nc.psum_tensor("M", [P, 2, BANK], F32))
        M2 = ctx.enter_context(nc.psum_tensor("M2", [P, BANK], F32))
        Mb = M2[:].bitcast(BF16)

        def four(n):
            return S[:, n, :] if n < 2 else Tp[:, n - 2, :]

        def xt_bank(v, set_up=False):
            if not set_up:
                return M[:, v % 2, :]
            if v < KC:
                return four(v)
            return O[:, :] if v % 2 == 0 else M2[:, :]

        def o_bank(i):
            return O[:, :] if i % 2 == 0 else M2[:, :]

        ident_ready = sem("ident_ready")
        consts_set = sem("consts_set")
        w2_loaded = sem("w2_loaded")
        table_loaded = sem("table_loaded")
        bias_loaded = sem("bias_loaded")
        b2_loaded = sem("b2_loaded")
        x0_loaded = [sem(f"x0_loaded{i}") for i in range(2 * NH)]
        w_loaded = [sem(f"w_loaded{i}") for i in range(4)]
        w_hi = sem("w_hi")
        w1_split = sem("w1_split")
        wq_split = sem("wq_split")
        w2_split = sem("w2_split")
        w2_zeroed = sem("w2_zeroed")
        table_zeroed = sem("table_zeroed")
        wk_split = sem("wk_split")
        table_step = sem("table_step")
        table_ready = sem("table_ready")
        a_full = sem("a_full")
        a_hi = sem("a_hi")
        a_split = sem("a_split")
        wv_full = sem("wv_full")
        wv_hi = sem("wv_hi")
        wv_split = sem("wv_split")
        x_loaded = [sem(f"x_loaded{i}") for i in range(2)]
        stats_done = sem("stats_done")
        moments_done = sem("moments_done")
        var_eps = sem("var_eps")
        rstd_done = sem("rstd_done")
        normed = sem("normed")
        xt_full = sem("xt_full")
        xt_hi = sem("xt_hi")
        xt_split = sem("xt_split")
        unit_full = sem("unit_full")
        act_done = sem("act_done")
        h_hi = sem("h_hi")
        h_split = sem("h_split")
        yv_hi = sem("yv_hi")
        yv_split = sem("yv_split")
        r_full = sem("r_full")
        r_copied = sem("r_copied")
        z_copied = sem("z_copied")
        rt_full = sem("rt_full")
        z_ready = sem("z_ready")
        gate_exp = sem("gate_exp")
        route = sem("route")
        route_sub = sem("route_sub")
        route_exp = sem("route_exp")
        onehot_ready = sem("onehot_ready")
        ot_full = sem("ot_full")
        ot_ready = sem("ot_ready")
        gathered = sem("gathered")
        scaled = sem("scaled")
        routed = sem("routed")
        tanh_done = sem("tanh_done")
        gate_ready = sem("gate_ready")
        s_full = sem("s_full")
        max_done = sem("max_done")
        negmax = sem("negmax")
        p_ready = sem("p_ready")
        pt_full = sem("pt_full")
        pt_hi = sem("pt_hi")
        pt_split = sem("pt_split")
        pv_half = sem("pv_half")
        o_full = sem("o_full")
        den_step = sem("den_step")
        f_done = sem("f_done")
        xres_loaded = [sem(f"xres_loaded{i}") for i in range(2)]
        out_built = sem("out_built")
        stored = sem("stored")

        setup = ExitStack()
        wraw = sb("wraw", [P, 3, KC, D], F32, setup)
        qs = [sb(f"Wq_{p}", [P, KC, D], F32R, setup) for p in ("hi", "lo")]
        ks = [sb(f"Wk_{p}", [P, KC, D], F32R, setup) for p in ("hi", "lo")]
        wvraw = sb("wvraw", [P, KC, D], F32, setup)
        setup.close()
        yT = [sb(f"yT_{p}", [P, KC, T], F32R) for p in ("hi", "lo")]
        V = [sb(f"V_{p}", [P, NT, D], F32R) for p in ("hi", "lo")]
        w2raw = th[:, 0:HC * LO].rearrange("p (c e) -> p c e", c=HC)
        traw = Pr[0:EC, :]

        first = 0
        SPLIT3 = ((0, 0), (0, 1), (1, 0))

        block = ctx.enter_context(nc.Block())

        @block.sync
        def _(sp):
            def load_stage(t, slot, free):
                sp.wait_ge(normed, free)
                sp.dma_start(xstage[:, slot, :], x_t[t] if isinstance(t, int) else
                             x_t[bass.ds(t, 1)].rearrange("a p d -> p (a d)")).then_inc(x_loaded[slot], 16)

            def load_res(t, slot):
                sp.dma_start(xres[:, slot, :], x_t[t] if isinstance(t, int) else
                             x_t[bass.ds(t, 1)].rearrange("a p d -> p (a d)")).then_inc(xres_loaded[slot], 16)

            def load_quarter(n):
                tiles = slice(n * TH // 2, (n + 1) * TH // 2)
                sp.dma_start(xn[:, tiles, :], x_t[tiles].rearrange("t p d -> p t d")).then_inc(x0_loaded[n], 16)

            def load_w(i, src, dst):
                sp.dma_start(dst, src.rearrange("(k p) d -> p k d", p=P)).then_inc(w_loaded[i], 16)

            load_quarter(0)
            load_quarter(1)
            for c in range(HC // 2):
                col = slice(c * P, (c + 1) * P)
                sp.dma_start(bcol[:, c:c + 1], b1[col].rearrange("(p o) -> p o", o=1)).then_inc(bias_loaded, 16)
                sp.dma_start(bcol[:, HC // 2 + c:HC // 2 + c + 1],
                             bg1[col].rearrange("(p o) -> p o", o=1)).then_inc(bias_loaded, 16)
            load_w(1, Wq, wraw[:, 1])
            sp.wait_ge(w2_zeroed, 1)
            for c in range(HC // 2):
                sp.dma_start(w2raw[:, c, 0:E], W2[c * P:(c + 1) * P, :]).then_inc(w2_loaded, 16)
                sp.dma_start(w2raw[:, HC // 2 + c, E:E + 1], Wg2[c * P:(c + 1) * P, :]).then_inc(w2_loaded, 16)
            load_w(2, Wk, wraw[:, 2])
            load_quarter(2)
            load_quarter(3)
            load_w(3, Wv, wvraw[:])
            sp.dma_start(b2g[:, 0:E], b2.partition_broadcast(P)).then_inc(b2_loaded, 16)
            sp.dma_start(b2g[:, E:E + 1], bg2.partition_broadcast(P)).then_inc(b2_loaded, 16)
            sp.wait_ge(table_zeroed, 1)
            for part in range(3):
                sp.dma_start(traw[32 * part:32 * part + E, 0:D], scales).then_inc(table_loaded, 16)
                sp.dma_start(traw[32 * part:32 * part + E, D:], biases).then_inc(table_loaded, 16)
            for t in range(2):
                load_res(t, t)

            def body(b, last):
                if not last:
                    load_stage(b * NT + NT, 0, b * NT + NT - 1)
                    load_stage(b * NT + NT + 1, 1, b * NT + NT)
                for i in range(NT):
                    if not last and i + 2 < NT:
                        load_stage(b * NT + NT + i + 2, i % 2, b * NT + NT + i + 1)
                    sp.wait_ge(out_built, b * NT + i + 1)
                    sp.dma_start(out_t[b * NT + i] if isinstance(b, int) else
                                 out_t[bass.ds(b * NT + i, 1)].rearrange("a p d -> p (a d)"),
                                 xres[:, i % 2, :]).then_inc(stored, 16)
                    if not (last and i >= NT - 2):
                        sp.wait_ge(stored, (b * NT + i + 1) * 16)
                        load_res(b * NT + i + 2, i % 2)

            body(first, False)
            with sp.Fori(1, B - 1) as b:
                body(b, False)
            body(B - 1, True)
            sp.wait_ge(stored, B * NT * 16)

        @block.gpsimd
        def _(pool):
            pool.memset(ident[:], 0.0).then_inc(consts_set, 1)
            pool.wait_ge(consts_set, 1)
            pool.affine_select(out=ident[:], in_=ident[:], compare_op=ALU.not_equal, fill=1.0, base=0,
                               pattern=[[-1, P]], channel_multiplier=1).then_inc(ident_ready, 1)
            pool.memset(epsc[:, 0, :], EPS)
            pool.memset(epsc[:, 1, :], -0.5).then_inc(consts_set, 1)
            pool.wait_ge(consts_set, 2)
            pool.wait_ge(ident_ready, 1)
            pool.tensor_copy(identb[:], ident[:]).then_inc(ident_ready, 1)
            pool.memset(traw, 0.0).then_inc(table_zeroed, 1)

            def invert_std(moments, n, tiles):
                pool.wait_ge(moments_done, moments)
                k = tiles.stop - tiles.start
                pool.tensor_tensor(rstd[:, 0, tiles], mv[:, tiles, 1], epsc[:, 0, 0:k], ALU.add).then_inc(var_eps, 1)
                pool.wait_ge(var_eps, n + 1)
                pool.tensor_tensor(rstd[:, 1, tiles], rstd[:, 0, tiles], epsc[:, 1, 0:k], ALU.pow).then_inc(rstd_done, 1)

            invert_std(TH, 0, slice(0, TH))
            pool.wait_ge(w_hi, 1)
            pool.tensor_tensor(w1g[1][:], wraw[:, 0], w1g[0][:].bitcast(F32), ALU.subtract).then_inc(w1_split, 1)
            invert_std(NT, 1, slice(TH, NT))
            pool.wait_ge(table_loaded, 16 * 6)
            pool.wait_ge(rstd_done, 2)
            steps = 0

            def step(ins):
                nonlocal steps
                ins.then_inc(table_step, 1)
                steps += 1
                pool.wait_ge(table_step, steps)

            step(pool.tensor_copy(table[:], traw))
            for part in (1, 2):
                for r in range(32 * part, EC, 32):
                    step(pool.tensor_tensor(traw[r:r + 32], traw[r:r + 32], table[r:r + 32, :], ALU.subtract))
                    step(pool.tensor_copy(table[r:r + 32, :], traw[r:r + 32]))
            pool.memset(epsc[:, 0, :], EPS).then_inc(table_ready, 1)

            def body(b):
                for i in range(NT):
                    n = b * NT + NT + i
                    invert_std(n + 1, b * NT + NH + i, slice(i, i + 1))

            body(first)
            with pool.Fori(1, B - 1) as b:
                body(b)

        @block.scalar
        def _(act):
            for src, cols in ((W1, slice(0, RH)), (Wg1, slice(RH, 2 * RH))):
                act.dma_start(wraw[:, 0, :, cols], src.rearrange("(k p) d -> p k d", p=P)).then_inc(w_loaded[0], 16)

            def split_hi(dst, src, done):
                act.activation(dst, src, ACT.Copy).then_inc(done, 1)

            def xt_units(n0, lot, half, set_up=False):
                for v in lot:
                    act.wait_ge(xt_full, n0 + v + 1)
                    split_hi(xnT[0][:, v % KC, half * BANK:half * BANK + BANK], xt_bank(v, set_up), xt_hi)

            for i, part, need in ((0, w1g, 32), (1, qs, 16), (2, ks, 16)):
                act.wait_ge(w_loaded[i], need)
                split_hi(part[0][:], wraw[:, i], w_hi)
                if i == 0:
                    xt_units(0, range(0, KC), 0, True)
            act.wait_ge(bias_loaded, 16 * HC)

            def set_up_between(u):
                if u == HC - 1:
                    for v in range(KC):
                        act.wait_ge(a_full, v + 1)
                        split_hi(A[0][:, v, :], four(v), a_hi)
                    xt_units(0, range(KC, XT_U), 1, True)
                elif HC <= u < HC + KC:
                    act.wait_ge(wv_full, u - HC + 1)
                    split_hi(WvT[0][:, u - HC, :], O[:, :], wv_hi)

            def softmax_exp(b, i):
                act.wait_ge(negmax, b * NT + i + 1)
                act.activation(Pr[:], S[:].rearrange("p n c -> p (n c)"), ACT.Exp, bias=mx[:, i % 2, 1:2],
                               scale=SCALE, accum_out=den[:, i % 2, 0:1]).then_inc(p_ready, 1)

            def gate_tanh(b, i):
                act.wait_ge(routed, b * NT + i + 1)
                act.activation(th, G[:, i % 2, :], ACT.Tanh, scale=0.5).then_inc(tanh_done, 1)

            def pt_unit(b, i, n):
                act.wait_ge(pt_full, (b * NT + i) * NH + n + 1)
                if i == NT - 1:
                    if n == 0:
                        act.wait_ge(pv_half, b + 1)
                    else:
                        act.wait_ge(o_full, b * NT + NT - 1)
                split_hi(PT[0][:, n * TH:(n + 1) * TH, :].rearrange("p t c -> p (t c)"), Tp[:, n, :], pt_hi)

            def body(b, last):
                for u, (kind, n, c) in enumerate(units):
                    act.wait_ge(unit_full, b * U + u + 1)
                    if kind == "h":
                        r = rank[u]
                        if r > 2:
                            act.wait_ge(h_split, b * H_U + r - 2)
                        act.activation(h[:, (r - 1) % 2, :], four(unit_at[u]), ACT.Relu if c < HC // 2 else ACT.Tanh,
                                       bias=bcol[:, c:c + 1]).then_inc(act_done, 1)
                        act.wait_ge(act_done, b * H_U + r)
                        split_hi(hs[0][:, (r - 1) % 2, :], h[:, (r - 1) % 2, :], h_hi)
                    elif kind == "y":
                        split_hi(yT[0][:, c, n * BANK:(n + 1) * BANK], four(unit_at[u]), yv_hi)
                    else:
                        split_hi(V[0][:, n, :], four(unit_at[u]), yv_hi)
                    if b is first:
                        set_up_between(u)
                    if u == last_h[1] + 3:
                        act.wait_ge(z_ready, b + 1)
                        act.activation(gt[:, 0, :], z[:, :, E], ACT.Exp, scale=-1.0).then_inc(gate_exp, 1)
                    if u == last_h[1] + 5:
                        act.wait_ge(route_sub, b + 1)
                        act.activation(rs[:], rs[:], ACT.Exp).then_inc(route_exp, 1)
                    if u == FIRST_SCORES:
                        act.wait_ge(ot_full, b + 1)
                        act.activation(onehotT[:], Mb[0:EC, :], ACT.Copy).then_inc(ot_ready, 1)
                        gate_tanh(b, 0)
                        softmax_exp(b, 0)
                xt0 = b * XT_U + XT_U
                for i in range(NT):
                    if i < NT - 1:
                        pt_unit(b, i, 0)
                        pt_unit(b, i, 1)
                        gate_tanh(b, i + 1)
                        softmax_exp(b, i + 1)
                    else:
                        if not last:
                            xt_units(xt0, range(0, 2), 0)
                        pt_unit(b, i, 0)
                        if not last:
                            xt_units(xt0, range(2, KC), 0)
                        pt_unit(b, i, 1)
                        if not last:
                            xt_units(xt0, range(KC, XT_U), 1)

            body(first, False)
            with act.Fori(1, B - 1) as b:
                body(b, False)
            body(B - 1, True)

        @block.vector
        def _(dve):
            def layernorm_moments(n, src, t):
                dve.bn_stats(st[:, t, :], src).then_inc(stats_done, 1)
                dve.wait_ge(stats_done, n + 1)
                dve.memset(sm[:, 3, 0:1], 0.0)
                dve.bn_aggr(mv[:, t, :], st[:, t, :]).then_inc(moments_done, 1)

            def layernorm_apply(src, t):
                dve.tensor_scalar(xn[:, t, :], src, mv[:, t, 0:1], rstd[:, 1, t:t + 1],
                                  ALU.subtract, ALU.mult).then_inc(normed, 1)

            def next_moments(b, t):
                dve.wait_ge(x_loaded[t % 2], b * (NT // 2 * 16) + (t // 2 + 1) * 16)
                layernorm_moments(b * NT + NT + t, xstage[:, t % 2, :], t)

            def next_apply(b, t):
                dve.wait_ge(rstd_done, b * NT + NH + t + 1)
                layernorm_apply(xstage[:, t % 2, :], t)

            def split_lo(dst, src, hi, done):
                dve.tensor_tensor(dst, src, hi.bitcast(F32), ALU.subtract).then_inc(done, 1)

            def xt_units(n0, lot, half, set_up=False):
                for v in lot:
                    dve.wait_ge(xt_hi, n0 + v + 1)
                    sl = slice(half * BANK, half * BANK + BANK)
                    split_lo(xnT[1][:, v % KC, sl], xt_bank(v, set_up), xnT[0][:, v % KC, sl], xt_split)

            dve.memset(w2raw, 0.0).then_inc(w2_zeroed, 1)
            for e in range(E):
                dve.memset(rev[:, e:e + 1], float(E - e))
            dve.memset(onehot[:], 0.0)
            dve.memset(w2s[:].bitcast(F32), 0.0).then_inc(w2_split, 1)

            def first_moments(half):
                for t in range(half * TH, (half + 1) * TH):
                    if t % (TH // 2) == 0:
                        dve.wait_ge(x0_loaded[t // (TH // 2)], 16)
                    dve.bn_stats(st[:, t, :], xn[:, t, :]).then_inc(stats_done, 1)
                dve.wait_ge(stats_done, (half + 1) * TH)
                dve.memset(sm[:, 3, 0:1], 0.0)
                for t in range(half * TH, (half + 1) * TH):
                    dve.bn_aggr(mv[:, t, :], st[:, t, :]).then_inc(moments_done, 1)

            def first_apply(half):
                dve.wait_ge(rstd_done, half + 1)
                for t in range(half * TH, (half + 1) * TH):
                    layernorm_apply(xn[:, t, :], t)

            first_moments(0)
            first_apply(0)
            xt_units(0, range(0, KC), 0, True)
            dve.wait_ge(w2_loaded, 16 * HC)
            dve.wait_ge(w2_split, 1)
            dve.tensor_copy(w2s[:, :, 0:LO], w2raw).then_inc(w2_split, 1)
            dve.wait_ge(w2_split, 2)
            split_lo(w2s[:, :, LO:2 * LO], w2raw, w2s[:, :, 0:LO], w2_split)
            dve.wait_ge(w_hi, 2)
            split_lo(qs[1][:], wraw[:, 1], qs[0][:], wq_split)
            dve.wait_ge(w_hi, 3)
            split_lo(ks[1][:], wraw[:, 2], ks[0][:], wk_split)

            def set_up_between(u):
                if u == 0:
                    first_moments(1)
                elif u == 1:
                    first_apply(1)
                elif u == HC - 1:
                    for v in range(KC):
                        dve.wait_ge(a_hi, v + 1)
                        split_lo(A[1][:, v, :], four(v), A[0][:, v, :], a_split)
                    xt_units(0, range(KC, XT_U), 1, True)
                elif HC <= u < HC + KC:
                    v = u - HC
                    dve.wait_ge(wv_hi, v + 1)
                    split_lo(WvT[1][:, v, :], O[:, :], WvT[0][:, v, :], wv_split)
                    if u == HC:
                        dve.wait_ge(b2_loaded, 32)

            ROUTE_SCORES, ROUTE_PICK = 5, 7

            def chain(done):
                def step(ins):
                    nonlocal done
                    ins.then_inc(route, 1)
                    done = done + 1
                    dve.wait_ge(route, done)
                return step

            def over_experts(row):
                return row.unsqueeze(2).to_broadcast([P, NT, E])

            def route_scores(b):
                step = chain(b * (ROUTE_SCORES + ROUTE_PICK))
                dve.wait_ge(z_copied, b * NH + 2)
                step(dve.tensor_tensor(z[:], Z[:, :, 0:E + 1], Z[:, :, LO:LO + E + 1], ALU.add))
                dve.tensor_tensor(z[:], z[:], b2g[:].unsqueeze(1).to_broadcast([P, NT, E + 1]),
                                  ALU.add).then_inc(z_ready, 1)
                dve.wait_ge(gate_exp, b + 1)
                step(dve.tensor_scalar(gt[:, 1, :], gt[:, 0, :], 1.0, None, ALU.add))
                step(dve.reciprocal(gt[:, 2, :], gt[:, 1, :]))
                step(dve.tensor_tensor(rs[:], z[:, :, 0:E], over_experts(gt[:, 2, :]), ALU.mult))
                step(dve.tensor_reduce(sm[:, 0, :], rs[:], AX.X, ALU.max))
                dve.tensor_tensor(rs[:], rs[:], over_experts(sm[:, 0, :]), ALU.subtract).then_inc(route_sub, 1)

            def route_pick(b):
                step = chain(b * (ROUTE_SCORES + ROUTE_PICK) + ROUTE_SCORES)
                dve.wait_ge(route_exp, b + 1)
                step(dve.tensor_reduce(sm[:, 1, :], rs[:], AX.X, ALU.add))
                step(dve.reciprocal(sm[:, 2, :], sm[:, 1, :]))
                step(dve.tensor_tensor(rs[:], rs[:], over_experts(sm[:, 2, :]), ALU.mult))
                step(dve.tensor_reduce(sm[:, 0, :], rs[:], AX.X, ALU.max))
                step(dve.tensor_tensor(rs[:], rs[:], over_experts(sm[:, 0, :]), ALU.is_ge))
                step(dve.tensor_tensor(rs[:], rs[:], rev[:].unsqueeze(1).to_broadcast([P, NT, E]), ALU.mult))
                step(dve.tensor_reduce(sm[:, 1, :], rs[:], AX.X, ALU.max))
                for part in range(3):
                    ins = dve.tensor_tensor(onehot[:, :, 32 * part:32 * part + E], rs[:], over_experts(sm[:, 1, :]), ALU.is_equal)
                ins.then_inc(onehot_ready, 1)

            def route_tile(b, i):
                dve.wait_ge(gathered, b * NT + i + 1)
                if i >= 2:
                    dve.wait_ge(out_built, b * NT + i - 1)
                dve.tensor_tensor(G[:, i % 2, :], M[:, 0, :], xn[:, i, :], ALU.mult).then_inc(scaled, 1)
                dve.wait_ge(scaled, b * NT + i + 1)
                dve.tensor_tensor(G[:, i % 2, :], G[:, i % 2, :], M[:, 1, :], ALU.add).then_inc(routed, 1)

            def gate_tile(b, i):
                dve.wait_ge(tanh_done, b * NT + i + 1)
                dve.scalar_tensor_tensor(out=G[:, i % 2, :], in0=th, scalar=1.0, in1=G[:, i % 2, :],
                                         op0=ALU.add, op1=ALU.mult).then_inc(gate_ready, 1)

            def softmax_max(b, i):
                dve.wait_ge(s_full, b * NT + i + 1)
                dve.tensor_reduce(mx[:, i % 2, 0:1], S[:].rearrange("p n c -> p (n c)"), AX.X, ALU.max).then_inc(max_done, 1)
                dve.wait_ge(max_done, b * NT + i + 1)
                dve.tensor_scalar(mx[:, i % 2, 1:2], mx[:, i % 2, 0:1], -SCALE, None, ALU.mult).then_inc(negmax, 1)

            def pt_unit(b, i, n):
                dve.wait_ge(pt_hi, (b * NT + i) * NH + n + 1)
                sl = slice(n * TH, (n + 1) * TH)
                split_lo(PT[1][:, sl, :].rearrange("p t c -> p (t c)"), Tp[:, n, :],
                         PT[0][:, sl, :].rearrange("p t c -> p (t c)"), pt_split)

            def finish_tile(b, i):
                dve.wait_ge(p_ready, b * NT + i + 1)
                dve.tensor_scalar(den[:, i % 2, 1:2], den[:, i % 2, 0:1], 2.0, None, ALU.mult).then_inc(den_step, 1)
                dve.wait_ge(den_step, (b * NT + i) * 2 + 1)
                dve.reciprocal(den[:, i % 2, 2:3], den[:, i % 2, 1:2]).then_inc(den_step, 1)
                dve.wait_ge(den_step, (b * NT + i) * 2 + 2)
                dve.wait_ge(gate_ready, b * NT + i + 1)
                dve.wait_ge(o_full, b * NT + i + 1)
                dve.scalar_tensor_tensor(out=G[:, i % 2, :], in0=o_bank(i), scalar=den[:, i % 2, 2:3], in1=G[:, i % 2, :],
                                         op0=ALU.mult, op1=ALU.mult).then_inc(f_done, 1)
                dve.wait_ge(f_done, b * NT + i + 1)
                dve.wait_ge(xres_loaded[i % 2], b * (NT // 2 * 16) + (i // 2 + 1) * 16)
                dve.tensor_tensor(xres[:, i % 2, :], G[:, i % 2, :], xres[:, i % 2, :], ALU.add).then_inc(out_built, 1)

            def body(b, last):
                for u, (kind, n, c) in enumerate(units):
                    r = rank[u]
                    if kind == "h":
                        dve.wait_ge(h_hi, b * H_U + r)
                        split_lo(hs[1][:, (r - 1) % 2, :], h[:, (r - 1) % 2, :], hs[0][:, (r - 1) % 2, :], h_split)
                    elif kind == "y":
                        dve.wait_ge(yv_hi, b * (Y_U + V_U) + r)
                        sl = slice(n * BANK, (n + 1) * BANK)
                        split_lo(yT[1][:, c, sl], four(unit_at[u]), yT[0][:, c, sl], yv_split)
                    else:
                        dve.wait_ge(yv_hi, b * (Y_U + V_U) + Y_U + r)
                        split_lo(V[1][:, n, :], four(unit_at[u]), V[0][:, n, :], yv_split)
                    if b is first:
                        set_up_between(u)
                    for half in range(NH):
                        if u == last_h[half] + 1:
                            dve.wait_ge(r_full, b * NH + half + 1)
                            dve.tensor_copy(Rs, M[:, half, :]).then_inc(r_copied, 1)
                        if u == last_h[half] + 2:
                            dve.wait_ge(rt_full, b * NH + half + 1)
                            src = (M2[:, :] if half == 0 else M[:, 0, :]).rearrange("p (t r) -> p t r", t=TH)
                            ins = dve.tensor_copy(Z[:, half * TH:(half + 1) * TH, :], src[:, :, 0:2 * LO])
                            ins.then_inc(z_copied, 1)
                    if u == last_h[1] + 3:
                        route_scores(b)
                    if u == last_h[1] + 5:
                        route_pick(b)
                    if u == FIRST_SCORES:
                        route_tile(b, 0)
                        if not last:
                            next_moments(b, 0)
                        gate_tile(b, 0)
                        softmax_max(b, 0)
                        if not last:
                            next_apply(b, 0)
                xt0 = b * XT_U + XT_U
                for i in range(NT):
                    if i < NT - 1:
                        if not last:
                            next_moments(b, i + 1)
                        pt_unit(b, i, 0)
                        pt_unit(b, i, 1)
                        route_tile(b, i + 1)
                        if not last:
                            next_apply(b, i + 1)
                        gate_tile(b, i + 1)
                        softmax_max(b, i + 1)
                        if i < NT - 2:
                            finish_tile(b, i)
                    else:
                        if not last:
                            xt_units(xt0, range(0, 2), 0)
                        pt_unit(b, i, 0)
                        if not last:
                            xt_units(xt0, range(2, KC), 0)
                        pt_unit(b, i, 1)
                        finish_tile(b, i - 1)
                        if not last:
                            xt_units(xt0, range(KC, XT_U), 1)
                        finish_tile(b, i)

            body(first, False)
            with dve.Fori(1, B - 1) as b:
                body(b, False)
            body(B - 1, True)

        @block.tensor
        def _(pe):
            def products(dst, chunks, stat, mov):
                for j, k in enumerate(chunks):
                    for s, (a, m) in enumerate(SPLIT3):
                        mm = pe.matmul(dst, stat(a, k), mov(m, k), start=(j == 0 and s == 0),
                                       stop=(j == len(chunks) - 1 and s == 2))
                return mm

            def xt_unit(n0, v, set_up=False):
                half, k = v // KC, v % KC
                if v >= 2 and not (set_up and v < KC + 2):
                    pe.wait_ge(xt_split, n0 + v - 1)
                for t in range(TH):
                    mm = pe.transpose(xt_bank(v, set_up)[:, t * P:(t + 1) * P], xn[:, half * TH + t, k * P:(k + 1) * P], ident[:])
                mm.then_inc(xt_full, 1)

            pe.wait_ge(ident_ready, 2)
            pe.wait_ge(normed, TH)
            for v in range(KC):
                xt_unit(0, v, True)
            pe.wait_ge(w1_split, 1)
            pe.wait_ge(w2_split, 3)

            def set_up_between(u):
                if u == HC - 1:
                    pe.wait_ge(wq_split, 1)
                    pe.wait_ge(wk_split, 1)
                    for v in range(KC):
                        pe.wait_ge(h_split, v + 1)
                        products(four(v), range(KC), lambda a, k: qs[a][:, k, v * P:(v + 1) * P],
                                 lambda m, k: ks[m][:, k, :]).then_inc(a_full, 1)
                    pe.wait_ge(normed, NT)
                    for v in range(KC, XT_U):
                        xt_unit(0, v, True)
                    pe.wait_ge(a_split, KC)
                elif HC <= u < HC + KC:
                    v = u - HC
                    if v == 0:
                        pe.wait_ge(w_loaded[3], 16)
                        pe.wait_ge(xt_split, XT_U)
                    else:
                        pe.wait_ge(wv_split, v)
                    for t in range(KC):
                        mm = pe.transpose(O[:, t * P:(t + 1) * P], wvraw[:, t, v * P:(v + 1) * P], ident[:])
                    mm.then_inc(wv_full, 1)
                elif u == U - V_U - 1:
                    pe.wait_ge(wv_split, KC)

            def w2_products(b, r):
                half, c = (r - 1) // HC, (r - 1) % HC
                pe.wait_ge(h_split, b * H_U + r)
                for part in range(2):
                    mm = pe.matmul(M[:, half, :], w2s[:, c, :], hs[part][:, (r - 1) % 2, :],
                                   start=(c == 0 and part == 0), stop=(c == HC - 1 and part == 1))
                if c == HC - 1:
                    mm.then_inc(r_full, 1)

            def turn_router(b, half):
                pe.wait_ge(r_copied, b * NH + half + 1)
                dst = M2[:, :] if half == 0 else M[:, 0, :]
                for t in range(TH):
                    mm = pe.transpose(dst[:, t * P:(t + 1) * P], Rs[:, t * P:(t + 1) * P], ident[:])
                mm.then_inc(rt_full, 1)

            def gather(b, i):
                if i:
                    pe.wait_ge(routed, b * NT + i)
                else:
                    pe.wait_ge(table_ready, 1)
                for n in range(2):
                    mm = pe.matmul(M[:, n, :], onehotT[:, i * P:(i + 1) * P], table[:, n * D:(n + 1) * D],
                                   start=True, stop=True)
                mm.then_inc(gathered, 1)

            def scores(b, i, n):
                mm = products(S[:, n, :], range(KC), lambda a, k: yT[a][:, k, i * P:(i + 1) * P],
                              lambda m, k: xnT[m][:, k, n * BANK:(n + 1) * BANK])
                if n == NH - 1:
                    mm.then_inc(s_full, 1)

            def turn_probs(b, i):
                pe.wait_ge(p_ready, b * NT + i + 1)
                for n in range(NH):
                    if i == NT - 1:
                        pe.wait_ge(pt_split, (b * NT + i - 1) * NH + n + 1)
                    for t in range(TH):
                        c = n * TH + t
                        mm = pe.transpose(Tp[:, n, t * P:(t + 1) * P], Pr[:, c * P:(c + 1) * P], ident[:])
                    mm.then_inc(pt_full, 1)

            def beside(b, i, c, last):
                if i == NT - 2 and c == TH:
                    turn_probs(b, NT - 1)
                if last:
                    return
                if i == NT - 2 and c in (2, 3, 5, 6):
                    v = (2, 3, 5, 6).index(c)
                    if v == 0:
                        pe.wait_ge(normed, b * NT + NT + TH)
                        pe.wait_ge(routed, b * NT + NT)
                    xt_unit(b * XT_U + XT_U, v)
                if i == NT - 1 and c in (1, 3, 5, 6):
                    v = KC + (1, 3, 5, 6).index(c)
                    if v == KC:
                        pe.wait_ge(normed, b * NT + 2 * NT)
                    xt_unit(b * XT_U + XT_U, v)

            def attend(b, i, last):
                for c in range(NT):
                    if c % TH == 0:
                        pe.wait_ge(pt_split, (b * NT + i) * NH + c // TH + 1)
                    for s, (a, m) in enumerate(SPLIT3):
                        mm = pe.matmul(o_bank(i), PT[a][:, c, :], V[m][:, c, :], start=(c == 0 and s == 0),
                                       stop=(c == NT - 1 and s == 2))
                    if c == NT - 1:
                        mm.then_inc(o_full, 1)
                    elif c == TH - 1 and i == NT - 2:
                        mm.then_inc(pv_half, 1)
                    beside(b, i, c, last)

            def body(b, last):
                def unit_read(u):
                    kind, r = units[u][0], rank[u]
                    if kind == "h":
                        pe.wait_ge(h_split, b * H_U + r)
                    else:
                        pe.wait_ge(yv_split, b * (Y_U + V_U) + r + (Y_U if kind == "v" else 0))

                for u, (kind, n, c) in enumerate(units):
                    if u == 0:
                        pe.wait_ge(xt_split, b * XT_U + KC)
                    if u == HC + KC:
                        pe.wait_ge(xt_split, b * XT_U + XT_U)
                    before = [w for w in range(u) if unit_at[w] == unit_at[u]]
                    if before:
                        unit_read(before[-1])
                    if kind == "h":
                        mm = products(four(unit_at[u]), range(KC), lambda a, k: w1g[a][:, k, c * P:(c + 1) * P],
                                      lambda m, k: xnT[m][:, k, n * BANK:(n + 1) * BANK])
                    elif kind == "y":
                        mm = products(four(unit_at[u]), range(KC), lambda a, k: A[a][:, k, c * P:(c + 1) * P],
                                      lambda m, k: xnT[m][:, k, n * BANK:(n + 1) * BANK])
                    else:
                        mm = products(four(unit_at[u]), range(KC), lambda a, k: xnT[a][:, k, n * P:(n + 1) * P],
                                      lambda m, k: WvT[m][:, k, :])
                    mm.then_inc(unit_full, 1)
                    if u and units[u - 1][0] == "h":
                        w2_products(b, rank[u - 1])
                    for half in range(NH):
                        if u == last_h[half] + 2:
                            turn_router(b, half)
                    if b is first:
                        set_up_between(u)
                    if u == FIRST_SCORES:
                        pe.wait_ge(onehot_ready, b + 1)
                        for t in range(NT):
                            mm = pe.transpose(Mb[0:EC, t * P:(t + 1) * P], onehot[:, t, :], identb[:])
                        mm.then_inc(ot_full, 1)
                        unit_read(U - V_U)
                        scores(b, 0, 0)
                        pe.wait_ge(ot_ready, b + 1)
                        gather(b, 0)
                        unit_read(U - V_U + 1)
                        scores(b, 0, 1)
                for i in range(NT):
                    if i + 1 < NT:
                        pe.wait_ge(p_ready, b * NT + i + 1)
                        scores(b, i + 1, 0)
                        if i == 0:
                            unit_read(U - 1)
                        turn_probs(b, i)
                        gather(b, i + 1)
                        scores(b, i + 1, 1)
                    attend(b, i, last)

            body(first, False)
            with pe.Fori(1, B - 1) as b:
                body(b, False)
            body(B - 1, True)


_INS = ["L0_attn_x", "L0_attn_Wq", "L0_attn_Wk", "L0_attn_Wv", "L0_ffn_W1", "L0_ffn_b1", "L0_ffn_W2", "L0_ffn_b2",
        "L0_ffn_Wg1", "L0_ffn_bg1", "L0_ffn_Wg2", "L0_ffn_bg2", "L0_ffn_expert_scales", "L0_ffn_expert_biases"]


def kernel(**inputs):
    import numpy as _np
    import concourse.bacc as _bacc
    from concourse import mybir as _mybir
    from concourse.bass_utils import run_bass_kernel_spmd as _run

    nc = _bacc.Bacc("TRN2", target_bir_lowering=False, num_devices=1)
    arrays, args = {}, []
    for name in _INS:
        a = _np.ascontiguousarray(inputs[name])
        arrays[name] = a
        args.append(nc.dram_tensor(name, a.shape, _mybir.dt.from_np(a.dtype), kind="ExternalInput").ap())
    shape = arrays["L0_attn_x"].shape
    args.append(nc.dram_tensor("out", shape, _mybir.dt.float32, kind="ExternalOutput").ap())
    routed_attention_block(nc, *args)
    r = _run(nc, [arrays], core_ids=[0])
    return r.results[0]["out"]
```
